# Optimizing a Trainium2 kernel written in Bass

```python
import numpy as np
import jax
import jax.numpy as jnp

def _softmax(x, axis=-1):
    return jax.nn.softmax(x, axis=axis)

def _gelu(x):
    return jax.nn.gelu(x, approximate=True)

def _silu(x):
    return jax.nn.silu(x)

def _sigmoid(x):
    return jax.nn.sigmoid(x)

def _layernorm(x, axis=-1, eps=1e-05):
    m = jnp.mean(x, axis=axis, keepdims=True)
    v = jnp.var(x, axis=axis, keepdims=True)
    return (x - m) / jnp.sqrt(v + eps)

def _scatter_add(tgt, idx, src, axis=0):
    return tgt.at[idx].add(src)

def _segment_sum(src, seg, n):
    return jax.ops.segment_sum(src, seg, n)
kernel_name = 'mk_recurrent_d1_jaxref_r8_9edaf7'

def setup_inputs(seed: int=0):
    np.random.seed(seed)
    _w = jnp.asarray

    def _L0_attn_setup():
        import jax, jax.numpy as jnp
        import numpy as np
        import math
        B, S, D = (1, 256, 512)
        H, KV, HD = (32, 8, 128)
        GROUPS = H // KV
        SYS_LEN, IMG_LEN = (35, 72)
        ENH, SUP = (1.5, 0.5)
        ROPE_BASE = 10000.0

        def _rope_cos_sin(seq_len, dtype):
            inv_freq = 1.0 / ROPE_BASE ** (jnp.arange(0, HD, 2, dtype=jnp.float32) / HD)
            pos = jnp.arange(seq_len, dtype=jnp.float32)
            freqs = pos[:, None] * inv_freq[None, :]
            emb = jnp.concatenate([freqs, freqs], axis=-1)
            return (jnp.cos(emb).astype(dtype), jnp.sin(emb).astype(dtype))

        def _rotate_half(x):
            x1, x2 = (x[..., :HD // 2], x[..., HD // 2:])
            return jnp.concatenate([-x2, x1], axis=-1)
        key = jax.random.key(seed)
        ks = jax.random.split(key, 5)
        scale = 0.02
        return {'hidden_states': jax.random.normal(ks[0], (B, S, D), dtype=jnp.float32), 'wq': jax.random.normal(ks[1], (H * HD, D), dtype=jnp.float32) * scale, 'wk': jax.random.normal(ks[2], (KV * HD, D), dtype=jnp.float32) * scale, 'wv': jax.random.normal(ks[3], (KV * HD, D), dtype=jnp.float32) * scale, 'wo': jax.random.normal(ks[4], (D, H * HD), dtype=jnp.float32) * scale}
    _L0_attn_in = _L0_attn_setup()

    def _L0_ffn_setup():
        import jax, jax.numpy as jnp
        import numpy as np
        LORA_SCALE = 16.0 / jnp.sqrt(16.0)
        TOP_K = 2
        key = jax.random.key(seed)
        k1, k2, k3, k4 = jax.random.split(key, 4)
        B_, S, D, O, E, R = (4, 256, 512, 512, 4, 16)
        x = jax.random.normal(k1, (B_, S, D), dtype=jnp.float32)
        router_w = jax.random.normal(k2, (E, D), dtype=jnp.float32) * 0.02
        A = jax.random.normal(k3, (E, R, D), dtype=jnp.float32) * 0.02
        B = jax.random.normal(k4, (O,), dtype=jnp.float32)
        B = jax.random.normal(k4, (E, O, R), dtype=jnp.float32) * 0.02
        return {'x': x, 'router_w': router_w, 'A': A, 'B': B}
    _L0_ffn_in = _L0_ffn_setup()
    _d = {'L0_attn_hidden_states': _L0_attn_in['hidden_states'], 'L0_attn_wq': _L0_attn_in['wq'], 'L0_attn_wk': _L0_attn_in['wk'], 'L0_attn_wv': _L0_attn_in['wv'], 'L0_attn_wo': _L0_attn_in['wo'], 'L0_ffn_router_w': _L0_ffn_in['router_w'], 'L0_ffn_A': _L0_ffn_in['A'], 'L0_ffn_B': _L0_ffn_in['B']}
    _x0 = _d['L0_attn_hidden_states']
    _d['L0_attn_hidden_states'] = jax.random.normal(jax.random.fold_in(jax.random.key(seed), 1), (8, 256, 512), dtype=_x0.dtype)
    del _x0
    return _d

def reference(L0_attn_hidden_states, L0_attn_wq, L0_attn_wk, L0_attn_wv, L0_attn_wo, L0_ffn_router_w, L0_ffn_A, L0_ffn_B):

    def _L0_attn_ref(hidden_states, wq, wk, wv, wo):
        import jax, jax.numpy as jnp
        import numpy as np
        import math
        B, S, D = (1, 256, 512)
        H, KV, HD = (32, 8, 128)
        GROUPS = H // KV
        SYS_LEN, IMG_LEN = (35, 72)
        ENH, SUP = (1.5, 0.5)
        ROPE_BASE = 10000.0

        def _rope_cos_sin(seq_len, dtype):
            inv_freq = 1.0 / ROPE_BASE ** (jnp.arange(0, HD, 2, dtype=jnp.float32) / HD)
            pos = jnp.arange(seq_len, dtype=jnp.float32)
            freqs = pos[:, None] * inv_freq[None, :]
            emb = jnp.concatenate([freqs, freqs], axis=-1)
            return (jnp.cos(emb).astype(dtype), jnp.sin(emb).astype(dtype))

        def _rotate_half(x):
            x1, x2 = (x[..., :HD // 2], x[..., HD // 2:])
            return jnp.concatenate([-x2, x1], axis=-1)
        bsz, q_len, _ = hidden_states.shape
        dt = hidden_states.dtype
        q = (hidden_states @ wq.T).reshape(bsz, q_len, H, HD).transpose(0, 2, 1, 3)
        k = (hidden_states @ wk.T).reshape(bsz, q_len, KV, HD).transpose(0, 2, 1, 3)
        v = (hidden_states @ wv.T).reshape(bsz, q_len, KV, HD).transpose(0, 2, 1, 3)
        cos, sin = _rope_cos_sin(q_len, dt)
        q = q * cos + _rotate_half(q) * sin
        k = k * cos + _rotate_half(k) * sin
        k = jnp.repeat(k, GROUPS, axis=1)
        v = jnp.repeat(v, GROUPS, axis=1)
        scores = jnp.einsum('bhqd,bhkd->bhqk', q, k) / math.sqrt(HD)
        kpos = jnp.arange(q_len)
        key_scale = jnp.where(kpos < SYS_LEN, SUP, jnp.where(kpos < SYS_LEN + IMG_LEN, ENH, 1.0)).astype(dt)
        qpos = jnp.arange(q_len)
        row_sel = (qpos >= SYS_LEN + IMG_LEN)[:, None]
        scale = jnp.where(row_sel, key_scale[None, :], jnp.ones((), dt))
        scores = scores * scale
        causal = jnp.where(qpos[:, None] >= kpos[None, :], 0.0, jnp.finfo(jnp.float32).min)
        scores = scores + causal.astype(dt)
        probs = jax.nn.softmax(scores.astype(jnp.float32), axis=-1).astype(dt)
        attn = jnp.einsum('bhqk,bhkd->bhqd', probs, v)
        attn = attn.transpose(0, 2, 1, 3).reshape(bsz, q_len, H * HD)
        return attn @ wo.T

    def _L0_ffn_ref(x, router_w, A, B):
        import jax, jax.numpy as jnp
        import numpy as np
        LORA_SCALE = 16.0 / jnp.sqrt(16.0)
        TOP_K = 2
        D = x.shape[-1]
        flat = x.reshape(-1, D)
        logits = flat @ router_w.T
        topk_vals, topk_idx = jax.lax.top_k(logits, TOP_K)
        sparse = jnp.full_like(logits, -jnp.inf)
        rows = jnp.arange(logits.shape[0])[:, None]
        sparse = sparse.at[rows, topk_idx].set(topk_vals)
        gates = jax.nn.softmax(sparse, axis=-1)
        mid = jnp.einsum('tf,erf->ter', flat, A)
        all_deltas = jnp.einsum('ter,eor->teo', mid, B) * LORA_SCALE
        delta = jnp.einsum('te,teo->to', gates, all_deltas)
        return delta.reshape(*x.shape[:-1], -1)
    x = L0_attn_hidden_states
    xn = _layernorm(x, axis=-1)
    s = _L0_attn_ref(xn, L0_attn_wq, L0_attn_wk, L0_attn_wv, L0_attn_wo)
    g = _silu(_L0_ffn_ref(xn, L0_ffn_router_w, L0_ffn_A, L0_ffn_B))
    x = x + s * g
    return x

_drawn_inputs = setup_inputs


def setup_inputs(seed=0):
    import zlib

    import numpy as np

    out = dict(_drawn_inputs(seed))
    spreads = {}
    factors = {'L0_attn_wq': 8.0,
     'L0_attn_wk': 8.0,
     'L0_attn_wv': 8.0,
     'L0_attn_wo': 8.0,
     'L0_ffn_router_w': 8.0,
     'L0_ffn_A': 8.0,
     'L0_ffn_B': 8.0}
    for name, (base, spread) in spreads.items():
        noise = np.random.default_rng([zlib.crc32(name.encode()), seed]).standard_normal(out[name].shape)
        drawn = base * np.exp(spread * noise) if base else spread * noise
        out[name] = jnp.asarray(drawn.astype(out[name].dtype))
    for name, factor in factors.items():
        out[name] = (out[name] * factor).astype(out[name].dtype)
    return out
```

```python
from contextlib import ExitStack

import numpy as np

import concourse.bass as bass
from concourse import mybir

F32 = mybir.dt.float32
F32R = mybir.dt.float32r
ALU = mybir.AluOpType
ACT = mybir.ActivationFunctionType
AX = mybir.AxisListType

P = 128
BATCHES, SEQ, DM = 8, 256, 512
HEADS, KV_HEADS, HD = 32, 8, 128
GROUP = HEADS // KV_HEADS
EXPERTS, RANK = 4, 16
LORA_SCALE = 16.0 / 16.0 ** 0.5
SYS_LEN, IMG_LEN, ENHANCE, SUPPRESS = 35, 72, 1.5, 0.5
ROPE_BASE = 10000.0
EPS = 1e-5

TOKENS = BATCHES * SEQ
TILES = TOKENS // P
BLOCK = 2 * SEQ
BLOCKS = TOKENS // BLOCK
BLOCK_TILES = BLOCK // P
UNITS = KV_HEADS * BLOCKS
ITEMS = 4 * UNITS
DC = DM // P
ROWS = P + SEQ
MASKED = 3.0e38

WK, WQ, WV, WO = 0, 1, 5, 6
CHUNKS = 10
AR = EXPERTS * RANK + EXPERTS

T_COSQ, T_SINQ, T_COSK, T_SINK, T_MASK, T_RATIO, T_IDENT = 0, 256, 512, 768, 1024, 1280, 1408
T_COLS = 1536

K, H0, H1, H2, H3 = range(5)
KINDS = ["k", "h0", "h1", "h2", "h3"]
BUF = {K: 0, H0: 1, H1: 0, H2: 1, H3: 1}
V, VT0, VT1 = 5, 6, 7


def build(nc, x, w_seq, a_r, b_t, tables, out):
    g_dram = nc.dram_tensor("gate_scratch", (TILES, P, DM), F32).ap()
    x_t = x.rearrange("(t p) d -> t p d", p=P)
    out_t = out.rearrange("(t p) d -> t p d", p=P)

    ctx = ExitStack()
    with ctx:
        def sb(name, shape, dt=F32, scope=ctx):
            return scope.enter_context(nc.sbuf_tensor(name, shape, dt))

        def pb(name, shape):
            return ctx.enter_context(nc.psum_tensor(name, shape, F32))

        def sem(name):
            return ctx.enter_context(nc.semaphore(name))

        xT_hi = sb("xT_hi", [P, DC, TOKENS], F32R)
        xT_lo = sb("xT_lo", [P, DC, TOKENS], F32R)
        y_sum = sb("y_sum", [P, TILES, DM])
        w_hi = sb("w_hi", [P, CHUNKS, 512], F32R)
        w_lo = sb("w_lo", [P, CHUNKS, 512], F32R)
        q_hi = sb("q_hi", [P, GROUP, BLOCK], F32R)
        q_lo = sb("q_lo", [P, GROUP, BLOCK], F32R)
        k_hi = sb("k_hi", [P, BLOCK], F32R)
        k_lo = sb("k_lo", [P, BLOCK], F32R)
        v_hi = sb("v_hi", [P, BLOCK_TILES, HD], F32R)
        v_lo = sb("v_lo", [P, BLOCK_TILES, HD], F32R)
        probs = sb("probs", [P, 2, ROWS])
        rot = sb("rot", [P, 2, BLOCK])
        cosx = sb("cosx", [P, 2, BLOCK])
        k_full = sb("k_full", [P, BLOCK])
        v_T = sb("v_T", [P, BLOCK])
        tab = sb("tab", [P, T_COLS])
        raw = sb("raw", [P, 2, 512])
        row_min = sb("row_min", [P, 4])
        row_sum = sb("row_sum", [P, 4])
        row_inv = sb("row_inv", [P, 4])
        zero = sb("zero", [P, 1])
        early = ExitStack()
        late = ExitStack()
        stats = sb("stats", [P, TILES, 6], F32, early)
        meanvar = sb("meanvar", [P, TILES, 2], F32, early)
        rstd = sb("rstd", [P, TILES], F32, early)
        minus_half = sb("minus_half", [P, TILES], F32, early)
        ar_raw = sb("ar_raw", [P, DC, AR], F32, early)
        ar_hi = sb("ar_hi", [P, DC, AR], F32R, early)
        ar_lo = sb("ar_lo", [P, DC, AR], F32R, early)
        bT = sb("bT", [EXPERTS * RANK, DM], F32, early)
        mid_T = sb("mid_T", [AR, BLOCK], F32, early)
        mid = sb("mid", [P, TILES, AR], F32, early)
        beats = sb("beats", [P, 6, TILES], F32, early)
        keep = sb("keep", [P, TILES, EXPERTS], F32, early)
        gate = sb("gate", [P, TILES, EXPERTS], F32, early)
        gmax = sb("gmax", [P, TILES], F32, early)
        gsum = sb("gsum", [P, TILES], F32, early)
        gm_T = sb("gm_T", [EXPERTS * RANK, BLOCK], F32, early)
        silu = sb("silu", [P, 2, DM], F32, early)
        early.close()
        attn_hi = sb("attn_hi", [P, GROUP, BLOCK], F32R, late)
        attn_lo = sb("attn_lo", [P, GROUP, BLOCK], F32R, late)
        pT_hi = sb("pT_hi", [P, 2, ROWS], F32R, late)
        pT_lo = sb("pT_lo", [P, 2, ROWS], F32R, late)
        ctx.push(late)

        ident = tab[:, T_IDENT:T_IDENT + P]

        bank_a = pb("bank_a", [P, 512])
        bank_b = pb("bank_b", [P, 512])
        s_ps = pb("s_ps", [P, 2, 512])
        t_ps = pb("t_ps", [P, 2, 512])
        pv_ps = pb("pv_ps", [P, 512])
        o_ps = pb("o_ps", [P, 512])

        tables_in = sem("tables_in")
        x_in = [sem(f"x_in{b}") for b in range(BLOCKS)]
        ffn_in = sem("ffn_in")
        stat_done = sem("stat_done")
        aggr_done = sem("aggr_done")
        vareps_done = sem("vareps_done")
        half_done = sem("half_done")
        rstd_done = sem("rstd_done")
        norm_done = sem("norm_done")
        xpose_done = sem("xpose_done")
        xhi_done = sem("xhi_done")
        xlo_done = sem("xlo_done")
        arhi_done = sem("arhi_done")
        ar_done = sem("ar_done")
        midT_ps = sem("midT_ps")
        midT_done = sem("midT_done")
        mid_ps = sem("mid_ps")
        mid_done = sem("mid_done")
        gate_step = sem("gate_step")
        gate_shift = sem("gate_shift")
        gate_exp = sem("gate_exp")
        gm_done = sem("gm_done")
        gmT_ps = sem("gmT_ps")
        gmT_done = sem("gmT_done")
        delta_done = sem("delta_done")
        tanh_done = sem("tanh_done")
        silu_done = sem("silu_done")
        gate_out = [sem(f"gate_out{i}") for i in range(2)]
        y_zero = sem("y_zero")
        raw_in = [sem(f"raw_in{i}") for i in range(2)]
        whi_done = sem("whi_done")
        zero_done = sem("zero_done")
        w_ready = [sem(f"w_ready{c}") for c in range(CHUNKS)]
        proj_done = [sem(f"proj_done_{k}") for k in KINDS + ["v", "vt0", "vt1"]]
        rot_done = [sem(f"rot_done_{k}") for k in KINDS]
        sin_done = [sem(f"sin_done_{k}") for k in KINDS]
        cos_done = [sem(f"cos_done_{k}") for k in KINDS]
        sum_done = [sem(f"sum_done_{k}") for k in KINDS]
        qhi_done = [sem(f"qhi_done_{k}") for k in KINDS]
        q_ready = [sem(f"q_ready_{k}") for k in KINDS]
        khi1_done = sem("khi1_done")
        k1_ready = sem("k1_ready")
        vT_done = sem("vT_done")
        vhi_done = [sem(f"vhi_done{b}") for b in range(2)]
        v_ready = [sem(f"v_ready{b}") for b in range(2)]
        scores_done = sem("scores_done")
        ratio_done = sem("ratio_done")
        masked_done = sem("masked_done")
        exp_done = sem("exp_done")
        inv_done = sem("inv_done")
        probs_ready = sem("probs_ready")
        pT_ps = sem("pT_ps")
        pThi_done = sem("pThi_done")
        pT_ready = sem("pT_ready")
        pv_done = sem("pv_done")
        attnhi_done = sem("attnhi_done")
        attn_ready = sem("attn_ready")
        o_done = sem("o_done")
        y_added = sem("y_added")
        xg_in = sem("xg_in")
        y_gated = sem("y_gated")
        y_final = sem("y_final")
        out_done = sem("out_done")

        block = ctx.enter_context(nc.Block())
        FINAL = UNITS - BLOCKS
        LAST = UNITS - 1

        def slots(eng, u):
            return {c: (4 * u + c if isinstance(u, int) else eng.snap(4 * u + c)) for c in range(-4, 6)}

        def units(eng, u):
            return [u + c if isinstance(u, int) or c == 0 else eng.snap(u + c) for c in range(3)]

        def is_unit(u, n):
            return isinstance(u, int) and u == n

        def value(eng, v):
            return v if isinstance(v, int) else eng.snap(v)

        @block.sync
        def _(sp):
            for b in range(BLOCKS):
                sp.dma_start(y_sum[:, BLOCK_TILES * b:BLOCK_TILES * (b + 1), :],
                             x_t[BLOCK_TILES * b:BLOCK_TILES * (b + 1), :, :].rearrange("t p d -> p t d"))\
                  .then_inc(x_in[b], 16)
                if b == 0:
                    sp.dma_start(tab[:, :], tables).then_inc(tables_in, 16)
                    for c in range(2):
                        sp.dma_start(raw[:, c, :], w_seq[c, :, :]).then_inc(raw_in[c], 16)
                    sp.dma_start(ar_raw[:, :, :], a_r).then_inc(ffn_in, 16)
                    sp.dma_start(bT[:, :], b_t).then_inc(ffn_in, 16)
            for c in range(2, WO):
                sp.wait_ge(w_ready[c - 2], 1)
                sp.dma_start(raw[:, c % 2, :], w_seq[c, :, :]).then_inc(raw_in[c % 2], 16)
            for c in range(WO, WO + 2):
                sp.wait_ge(w_ready[c - 2], 1)
                sp.dma_start(raw[:, c % 2, :], w_seq[c, :, :]).then_inc(raw_in[c % 2], 16)
            for t in range(TILES):
                sp.wait_ge(silu_done, t + 1)
                sp.dma_start(g_dram[t, :, :], silu[:, t % 2, :]).then_inc(gate_out[t % 2], 16)

            def load_chunk(g, c):
                before = (c - 2) % CHUNKS
                sp.wait_ge(w_ready[before], value(sp, g + 1 if c >= 2 else g))
                sp.dma_start(raw[:, c % 2, :], w_seq[value(sp, g * CHUNKS + c), :, :]).then_inc(raw_in[c % 2], 16)

            with sp.Fori(0, KV_HEADS - 1) as g:
                for c in range(WO + 2, CHUNKS):
                    load_chunk(g, c)
                g_next = sp.snap(g + 1)
                for c in range(WO + 2):
                    load_chunk(g_next, c)
            for c in range(WO + 2, CHUNKS):
                load_chunk(KV_HEADS - 1, c)
            for r in range(2):
                sp.wait_ge(gate_out[r], 16 * TILES // 2)
            for c in range(CHUNKS - 2, CHUNKS):
                sp.wait_ge(w_ready[c], KV_HEADS)
            with sp.Fori(0, TILES) as t:
                sp.dma_start(raw[:, 0, :], x_t[t, :, :]).then_inc(xg_in, 16)
                sp.dma_start(raw[:, 1, :], g_dram[t, :, :]).then_inc(xg_in, 16)
                sp.wait_ge(y_final, value(sp, t + 1))
                sp.dma_start(out_t[t, :, :], y_sum[:, t, :]).then_inc(out_done, 16)
            sp.wait_ge(out_done, 16 * TILES)

        @block.gpsimd
        def _(pool):
            nc.gpsimd.memset(minus_half[:, :], -0.5).then_inc(half_done, 1)
            nc.gpsimd.memset(zero[:, :], 0.0).then_inc(zero_done, 1)
            pool.wait_ge(half_done, 1)
            pool.wait_ge(zero_done, 1)

            def inverse_std(b):
                s = slice(BLOCK_TILES * b, BLOCK_TILES * (b + 1))
                pool.wait_ge(vareps_done, b + 1)
                nc.gpsimd.tensor_tensor(rstd[:, s], meanvar[:, s, 1], minus_half[:, s], ALU.pow).then_inc(rstd_done, 1)

            def split(g, c):
                r = c % 2
                pool.wait_ge(raw_in[r], value(pool, 16 * (CHUNKS // 2 * g + c // 2 + 1)))
                nc.gpsimd.tensor_tensor(w_hi[:, c, :], raw[:, r, :], zero[:, 0:1].to_broadcast([P, 512]),
                                        ALU.add).then_inc(whi_done, 1)
                pool.wait_ge(whi_done, value(pool, CHUNKS * g + c + 1))
                nc.gpsimd.tensor_tensor(w_lo[:, c, :], raw[:, r, :], w_hi[:, c, :].bitcast(F32),
                                        ALU.subtract).then_inc(w_ready[c], 1)

            def sin_product(kind, count):
                s = T_SINK if kind == K else T_SINQ
                v = rot[:, BUF[kind], :].rearrange("p (b t) -> p b t", b=2)
                pool.wait_ge(rot_done[kind], count)
                nc.gpsimd.tensor_tensor(v, v, tab[:, s:s + SEQ].unsqueeze(1).to_broadcast([P, 2, SEQ]),
                                        ALU.mult).then_inc(sin_done[kind], 1)

            pool.wait_ge(tables_in, 16)
            for b in range(BLOCKS):
                inverse_std(b)
                split(0, b)
            for c in range(BLOCKS, WO):
                split(0, c)
            for kind in (K, H0, H1, H2):
                sin_product(kind, 1)
            pool.wait_ge(xpose_done, TILES)
            nc.gpsimd.memset(y_sum[:, :, :], 0.0).then_inc(y_zero, 1)

            def group(g, g_next):
                u0 = value(pool, 4 * g)
                for i in range(BLOCKS):
                    last = g_next is None and i == BLOCKS - 1
                    own = value(pool, u0 + i + 1)
                    ahead = None if last else value(pool, u0 + i + 2)
                    for j in range(4):
                        if j == 0:
                            sin_product(H3, own)
                        elif not last:
                            sin_product((K, H0, H1)[j - 1], ahead)
                        if i == 0 and j == 2:
                            pool.wait_ge(pv_done, value(pool, TILES * g + 2))
                            for c in range(WO, WO + 3):
                                split(g, c)
                        if i == 0 and j == 3:
                            split(g, WO + 3)
                        if j == 3 and not last:
                            sin_product(H2, ahead)
                        if g_next is None:
                            continue
                        used = value(pool, 4 * g + 4) if (i, j) in ((2, 2), (2, 3), (3, 0), (3, 1), (3, 2)) else None
                        if (i, j) == (2, 2):
                            pool.wait_ge(proj_done[K], used)
                            split(g_next, WK)
                        elif (i, j) in ((2, 3), (3, 0), (3, 1)):
                            h = {(2, 3): 0, (3, 0): 1, (3, 1): 2}[i, j]
                            pool.wait_ge(proj_done[H0 + h], used)
                            split(g_next, WQ + h)
                        elif (i, j) == (3, 2):
                            pool.wait_ge(proj_done[H3], used)
                            split(g_next, WQ + 3)
                            pool.wait_ge(proj_done[V], used)
                            split(g_next, WV)

            with pool.Fori(0, KV_HEADS - 1) as g:
                group(g, pool.snap(g + 1))
            group(KV_HEADS - 1, None)

        def three_pass(dst, w, x0):
            for c in range(DC):
                for n, (a, x) in enumerate(((0, xT_hi), (0, xT_lo), (1, xT_hi))):
                    mm = nc.tensor.matmul(dst, w(a, c), x[:, c, bass.ds(x0, BLOCK)], start=(c == 0 and n == 0),
                                          stop=(c == DC - 1 and n == 2))
            return mm

        def project(kind, bank, chunk, x0, weights):
            nc.tensor.wait_ge(w_ready[chunk], weights)
            three_pass(bank[:, :], lambda w, c: (w_hi, w_lo)[w][:, chunk, c * P:(c + 1) * P], x0)\
                .then_inc(proj_done[kind], 1)

        def scores(b, hp):
            for h in range(2):
                for qt in range(2):
                    q = slice(SEQ * b + P * qt, SEQ * b + P * (qt + 1))
                    keys = slice(SEQ * b, SEQ * b + P * (qt + 1))
                    dst = s_ps[:, h, P * qt:P * qt + P * (qt + 1)]
                    for n, (a, k) in enumerate(((q_hi, k_hi), (q_hi, k_lo), (q_lo, k_hi))):
                        mm = nc.tensor.matmul(dst, a[:, 2 * hp + h, q], k[:, keys], start=(n == 0), stop=(n == 2))
            mm.then_inc(scores_done, 1)

        def prob_value(at, j, v_count, first_items=False):
            pe = nc.tensor
            b = ((j - 1) % 4) // 2
            pe.wait_ge(pT_ready, at(0))
            pe.wait_ge(v_ready[b], v_count)
            if not first_items:
                pe.wait_ge(attn_ready, at(-1))
            full = pv_ps[:, :].rearrange("p (h q) -> p h q", h=2)
            steps = [(full, v_hi, 0, pT_hi, 0), (full[:, :, P:], v_hi, 1, pT_hi, SEQ), (full[:, :, P:], v_hi, 1, pT_lo, SEQ),
                     (full[:, :, P:], v_lo, 1, pT_hi, SEQ), (full, v_hi, 0, pT_lo, 0), (full, v_lo, 0, pT_hi, 0)]
            for i, (dst, v, kb, p, c) in enumerate(steps):
                mm = nc.tensor.matmul(dst, v[:, 2 * b + kb, :], p[:, :, c:c + (P if kb else SEQ)], start=(i == 0), stop=(i == 5))
            mm.then_inc(pv_done, 1)

        def output_tile(at, j, first_tile=False):
            pe = nc.tensor
            b, t = ((j - 3) % 4) // 2, ((j - 3) % 4) % 2
            pe.wait_ge(attn_ready, at(-1 if t == 0 else -2))
            if not first_tile:
                pe.wait_ge(y_added, at(-3))
            rows = slice(SEQ * b + P * t, SEQ * b + P * (t + 1))
            for h in range(GROUP):
                for i, (a, w) in enumerate(((attn_hi, w_hi), (attn_hi, w_lo), (attn_lo, w_hi))):
                    mm = nc.tensor.matmul(o_ps[:, :], a[:, h, rows], w[:, WO + h, :], start=(h == 0 and i == 0),
                                          stop=(h == GROUP - 1 and i == 2))
            mm.then_inc(o_done, 1)

        def pe_unit(u):
            pe = nc.tensor
            first, last = is_unit(u, 0), is_unit(u, LAST)
            c0, c1, c2 = units(pe, u)
            n4 = slots(pe, u)
            x_own = value(pe, (u % BLOCKS) * BLOCK)
            x_next = value(pe, ((u + 1) % BLOCKS) * BLOCK)
            w_own = value(pe, u // BLOCKS + 1)
            w_next = value(pe, (u + 1) // BLOCKS + 1)
            for j in range(4):
                n = n4[j]
                if j == 0:
                    pe.wait_ge(cos_done[H1], c1)
                    pe.wait_ge(cos_done[H2], c1)
                    project(H3, bank_a, WQ + 3, x_own, w_own)
                    project(V, bank_b, WV, x_own, w_own)
                elif j in (1, 2):
                    pe.wait_ge(vT_done, c1)
                    if j == 1:
                        pe.wait_ge(cos_done[H3], c1)
                    else:
                        pe.wait_ge(v_ready[0], c1)
                    for kb in range(2):
                        t = 2 * (j - 1) + kb
                        mm = nc.tensor.transpose(bank_a[:, kb * P:(kb + 1) * P], v_T[:, t * P:(t + 1) * P], ident)
                    mm.then_inc(proj_done[VT0 if j == 1 else VT1], 1)
                    if not last:
                        if j == 1:
                            project(K, bank_b, WK, x_next, w_next)
                        else:
                            pe.wait_ge(cos_done[K], c2)
                            project(H0, bank_b, WQ, x_next, w_next)
                elif not last:
                    pe.wait_ge(v_ready[1], c1)
                    project(H1, bank_a, WQ + 1, x_next, w_next)
                    pe.wait_ge(cos_done[H0], c2)
                    project(H2, bank_b, WQ + 2, x_next, w_next)
                if not (first and j < 3):
                    if j == 3:
                        for h in range(GROUP):
                            pe.wait_ge(w_ready[WO + h], w_own)
                    output_tile(lambda c: n4[j + c], j, first_tile=first)
                if not (first and j == 0):
                    prob_value(lambda c: n4[j + c], j, v_count=c1 if j > 0 else c0, first_items=first and j == 1)
                pe.wait_ge(probs_ready, n4[j + 1])
                if not (first and j == 0):
                    pe.wait_ge(pT_ready, n)
                for h in range(2):
                    for s in range(ROWS // P):
                        mm = nc.tensor.transpose(t_ps[:, h, s * P:(s + 1) * P], probs[:, h, s * P:(s + 1) * P], ident)
                mm.then_inc(pT_ps, 1)
                if not (last and j == 3):
                    pe.wait_ge(masked_done, n4[j + 1])
                    if j == 0:
                        pe.wait_ge(q_ready[H2], c1)
                        pe.wait_ge(q_ready[H3], c1)
                    elif j == 1:
                        pe.wait_ge(k1_ready, c1)
                    elif j == 3:
                        for kind in (K, H0, H1):
                            pe.wait_ge(q_ready[kind], c2)
                    scores(b=((j + 1) % 4) // 2, hp=(j + 1) % 2)

        @block.tensor
        def _(pe):
            pe.wait_ge(tables_in, 16)
            for t in range(TILES):
                bank = (bank_a, bank_b)[t % 2]
                pe.wait_ge(norm_done, t + 1)
                if t >= 2:
                    pe.wait_ge(xlo_done, t - 1)
                for c in range(DC):
                    mm = nc.tensor.transpose(bank[:, c * P:(c + 1) * P], y_sum[:, t, c * P:(c + 1) * P], ident)
                mm.then_inc(xpose_done, 1)
            pe.wait_ge(ar_done, 1)
            pe.wait_ge(xlo_done, TILES)
            for b in range(BLOCKS):
                if b >= 1:
                    pe.wait_ge(midT_done, b)
                three_pass(o_ps[0:AR, :], lambda w, c: (ar_hi, ar_lo)[w][:, c, :], BLOCK * b).then_inc(midT_ps, 1)
                pe.wait_ge(midT_done, b + 1)
                if b >= 2:
                    pe.wait_ge(mid_done, b - 1)
                for t in range(BLOCK_TILES):
                    mm = nc.tensor.transpose(t_ps[:, b % 2, AR * t:AR * (t + 1)], mid_T[:, t * P:(t + 1) * P],
                                             ident[0:AR, 0:AR])
                mm.then_inc(mid_ps, 1)
            pe.wait_ge(gm_done, 1)
            pe.wait_ge(ffn_in, 32)
            for b in range(BLOCKS):
                if b >= 1:
                    pe.wait_ge(gmT_done, b)
                for t in range(BLOCK_TILES):
                    mm = nc.tensor.transpose(pv_ps[0:EXPERTS * RANK, t * P:(t + 1) * P],
                                             mid[:, BLOCK_TILES * b + t, 0:EXPERTS * RANK], ident)
                mm.then_inc(gmT_ps, 1)
                pe.wait_ge(gmT_done, b + 1)
                for t in range(BLOCK_TILES):
                    n = BLOCK_TILES * b + t
                    if n >= 2:
                        pe.wait_ge(silu_done, n - 1)
                    nc.tensor.matmul((bank_a, bank_b)[n % 2][:, :], gm_T[:, t * P:(t + 1) * P], bT[:, :],
                                     start=True, stop=True).then_inc(delta_done, 1)
            pe.wait_ge(silu_done, TILES)
            project(K, bank_b, WK, 0, 1)
            pe.wait_ge(cos_done[K], 1)
            project(H0, bank_b, WQ, 0, 1)
            project(H1, bank_a, WQ + 1, 0, 1)
            pe.wait_ge(cos_done[H0], 1)
            project(H2, bank_b, WQ + 2, 0, 1)
            for kind in (K, H0, H1):
                pe.wait_ge(q_ready[kind], 1)
            scores(0, 0)
            pe_unit(0)
            with pe.Fori(1, LAST) as u:
                pe_unit(u)
            pe_unit(LAST)
            n = 4 * UNITS
            for m in range(n, n + 3):
                output_tile(lambda c: m + c, m % 4)
                if m == n:
                    prob_value(lambda c: m + c, 0, v_count=UNITS)

        def swap_halves(kind, bank, count, before, before_count):
            act = nc.scalar
            act.wait_ge(proj_done[kind], count)
            if before is not None:
                act.wait_ge(sum_done[before], before_count)
            r = rot[:, BUF[kind], :]
            half = HD // 2
            nc.scalar.activation(r[0:half, :], bank[half:HD, :], ACT.Copy)
            nc.scalar.activation(r[half:HD, :], bank[0:half, :], ACT.Copy).then_inc(rot_done[kind], 1)

        def q_high(kind, count, used):
            act = nc.scalar
            act.wait_ge(sum_done[kind], count)
            if used is not None:
                act.wait_ge(scores_done, used)
            nc.scalar.activation(q_hi[:, kind - H0, :], cosx[:, BUF[kind], :], ACT.Copy).then_inc(qhi_done[kind], 1)

        def k_high(b, count, used):
            act = nc.scalar
            act.wait_ge(sum_done[K], count)
            if used is not None:
                act.wait_ge(scores_done, used)
            s = slice(SEQ * b, SEQ * (b + 1))
            nc.scalar.activation(k_hi[:, s], k_full[:, s], ACT.Copy).then_inc((qhi_done[K], khi1_done)[b], 1)

        def v_high(b, count, used):
            act = nc.scalar
            act.wait_ge(proj_done[VT0 + b], count)
            if used is not None:
                act.wait_ge(pv_done, used)
            nc.scalar.activation(v_hi[:, 2 * b:2 * b + 2, :], bank_a[:, 0:SEQ].rearrange("p (k d) -> p k d", k=2),
                                 ACT.Copy).then_inc(vhi_done[b], 1)

        def attn_high(n, j, old=None):
            act = nc.scalar
            i = (j - 1) % 4
            act.wait_ge(pv_done, n)
            if old is not None:
                act.wait_ge(o_done, old)
            nc.scalar.activation(attn_hi[:, 2 * (i % 2):2 * (i % 2) + 2, SEQ * (i // 2):SEQ * (i // 2 + 1)],
                                 pv_ps[:, :].rearrange("p (h q) -> p h q", h=2), ACT.Copy).then_inc(attnhi_done, 1)

        def act_unit(u):
            act = nc.scalar
            first, last = is_unit(u, 0), is_unit(u, LAST)
            c0, c1, c2 = units(act, u)
            n4 = slots(act, u)
            for j in range(4):
                n = n4[j]
                act.wait_ge(masked_done, n4[j + 1])
                for h in range(2):
                    for qt in range(2):
                        s = probs[:, h, P * qt:P * qt + P * (qt + 1)]
                        i = 2 * h + qt
                        a = nc.scalar.activation(s, s, ACT.Exp, bias=row_min[:, i:i + 1], scale=-1.0,
                                                 accum_out=row_sum[:, i:i + 1])
                a.then_inc(exp_done, 1)
                if j == 0:
                    swap_halves(H3, bank_a, c1, H2, c1)
                    act.wait_ge(proj_done[V], c1)
                    if not first:
                        act.wait_ge(proj_done[VT1], c0)
                    nc.scalar.activation(v_T[:, :], bank_b[:, :], ACT.Copy).then_inc(vT_done, 1)
                    q_high(H3, c1, None if first else n4[0])
                elif j == 1:
                    v_high(0, c1, None if first else n4[-2])
                    if not last:
                        swap_halves(K, bank_b, c2, H1, c1)
                        k_high(0, c2, n4[2])
                elif j == 2:
                    v_high(1, c1, None if first else n4[0])
                    if not last:
                        swap_halves(H0, bank_b, c2, H3, c1)
                        q_high(H0, c2, n4[3])
                elif not last:
                    k_high(1, c2, n4[4])
                    swap_halves(H1, bank_a, c2, K, c2)
                    swap_halves(H2, bank_b, c2, H0, c2)
                    q_high(H1, c2, n4[3])
                    q_high(H2, c2, n4[4])
                if not (first and j == 0):
                    attn_high(n, j, None if first else n4[(-3, -2, -2, 0)[j]])
                act.wait_ge(pT_ps, n4[j + 1])
                if not (first and j == 0):
                    act.wait_ge(pv_done, n)
                nc.scalar.activation(pT_hi[:, :, :], t_ps[:, :, 0:ROWS], ACT.Copy).then_inc(pThi_done, 1)

        @block.scalar
        def _(act):
            for t in range(TILES):
                act.wait_ge(xpose_done, t + 1)
                nc.scalar.activation(xT_hi[:, :, t * P:(t + 1) * P],
                                     (bank_a, bank_b)[t % 2][:, :].rearrange("p (c t) -> p c t", c=DC),
                                     ACT.Copy).then_inc(xhi_done, 1)
            for b in range(BLOCKS):
                act.wait_ge(midT_ps, b + 1)
                if b >= 1:
                    act.wait_ge(mid_ps, b)
                nc.scalar.activation(mid_T[:, :], o_ps[0:AR, :], ACT.Copy).then_inc(midT_done, 1)
            act.wait_ge(gate_shift, 1)
            nc.scalar.activation(gate[:, :, :], gate[:, :, :], ACT.Exp).then_inc(gate_exp, 1)
            for b in range(BLOCKS):
                act.wait_ge(gmT_ps, b + 1)
                if b >= 1:
                    act.wait_ge(delta_done, BLOCK_TILES * b)
                nc.scalar.activation(gm_T[:, :], pv_ps[0:EXPERTS * RANK, :], ACT.Copy).then_inc(gmT_done, 1)
                for t in range(BLOCK_TILES * b, BLOCK_TILES * (b + 1)):
                    act.wait_ge(delta_done, t + 1)
                    if t >= 2:
                        act.wait_ge(gate_out[t % 2], 16 * (t // 2))
                    nc.scalar.activation(silu[:, t % 2, :], (bank_a, bank_b)[t % 2][:, :],
                                         ACT.Tanh).then_inc(tanh_done, 1)
            swap_halves(K, bank_b, 1, None, None)
            swap_halves(H0, bank_b, 1, None, None)
            k_high(0, 1, None)
            q_high(H0, 1, None)
            swap_halves(H1, bank_a, 1, K, 1)
            q_high(H1, 1, None)
            swap_halves(H2, bank_b, 1, H0, 1)
            q_high(H2, 1, None)
            k_high(1, 1, None)
            for r in range(2):
                act.wait_ge(gate_out[r], 16 * TILES // 2)
            act_unit(0)
            with act.Fori(1, LAST) as u:
                act_unit(u)
            act_unit(LAST)
            attn_high(4 * UNITS, 0)

        def normalise(b):
            dve = nc.vector
            dve.wait_ge(rstd_done, b + 1)
            for t in range(BLOCK_TILES * b, BLOCK_TILES * (b + 1)):
                nc.vector.tensor_scalar(y_sum[:, t, :], y_sum[:, t, :], meanvar[:, t, 0:1], rstd[:, t:t + 1],
                                        ALU.subtract, ALU.mult).then_inc(norm_done, 1)
            for t in range(BLOCK_TILES * b, BLOCK_TILES * (b + 1)):
                s = slice(t * P, (t + 1) * P)
                dve.wait_ge(xhi_done, t + 1)
                nc.vector.tensor_tensor(xT_lo[:, :, s], (bank_a, bank_b)[t % 2][:, :].rearrange("p (c t) -> p c t", c=DC),
                                        xT_hi[:, :, s].bitcast(F32), ALU.subtract).then_inc(xlo_done, 1)

        def route(dve):
            steps = [0]

            def link(ins):
                steps[0] += 1
                ins.then_inc(gate_step, 1)
                dve.wait_ge(gate_step, steps[0])

            logit = lambda e: mid[:, :, EXPERTS * RANK + e]
            pairs = [(0, 1), (0, 2), (0, 3), (1, 2), (1, 3), (2, 3)]
            c = {p: beats[:, i, :] for i, p in enumerate(pairs)}
            for a, b in pairs:
                ins = nc.vector.tensor_tensor(c[a, b], logit(a), logit(b), ALU.is_ge)
            link(ins)
            tt = nc.vector.tensor_tensor
            tt(keep[:, :, 0], c[0, 1], c[0, 2], ALU.add)
            tt(keep[:, :, 1], c[1, 2], c[1, 3], ALU.add)
            tt(keep[:, :, 2], c[2, 3], c[0, 2], ALU.subtract)
            link(tt(keep[:, :, 3], c[0, 3], c[1, 3], ALU.add))
            tt(keep[:, :, 0], keep[:, :, 0], c[0, 3], ALU.add)
            tt(keep[:, :, 1], keep[:, :, 1], c[0, 1], ALU.subtract)
            tt(keep[:, :, 2], keep[:, :, 2], c[1, 2], ALU.subtract)
            link(tt(keep[:, :, 3], keep[:, :, 3], c[2, 3], ALU.add))
            ts = nc.vector.tensor_scalar
            ts(keep[:, :, 0], keep[:, :, 0], 2.0, None, ALU.is_ge)
            ts(keep[:, :, 1], keep[:, :, 1], 0.5, None, ALU.is_ge)
            ts(keep[:, :, 2], keep[:, :, 2], -0.5, None, ALU.is_ge)
            ts(keep[:, :, 3], keep[:, :, 3], 1.5, None, ALU.is_lt)
            logits = mid[:, :, EXPERTS * RANK:AR]
            link(nc.vector.tensor_reduce(gmax[:, :], logits, AX.X, ALU.max))
            wide = lambda v: v.unsqueeze(2).to_broadcast([P, TILES, EXPERTS])
            tt(gate[:, :, :], logits, wide(gmax[:, :]), ALU.subtract).then_inc(gate_shift, 1)
            dve.wait_ge(gate_exp, 1)
            link(tt(gate[:, :, :], gate[:, :, :], keep[:, :, :], ALU.mult))
            link(nc.vector.tensor_reduce(gsum[:, :], gate[:, :, :], AX.X, ALU.add))
            link(nc.vector.reciprocal(gsum[:, :], gsum[:, :]))
            link(ts(gsum[:, :], gsum[:, :], LORA_SCALE / 2, None, ALU.mult))
            link(tt(gate[:, :, :], gate[:, :, :], wide(gsum[:, :]), ALU.mult))
            for e in range(EXPERTS):
                m = mid[:, :, RANK * e:RANK * (e + 1)]
                ins = tt(m, m, gate[:, :, e].unsqueeze(2).to_broadcast([P, TILES, RANK]), ALU.mult)
            ins.then_inc(gm_done, 1)

        def cos_product(kind, bank, count):
            s = T_COSK if kind == K else T_COSQ
            nc.vector.wait_ge(rot_done[kind], count)
            nc.vector.tensor_tensor(cosx[:, BUF[kind], :].rearrange("p (b t) -> p b t", b=2),
                                    bank[:, :].rearrange("p (b t) -> p b t", b=2),
                                    tab[:, s:s + SEQ].unsqueeze(1).to_broadcast([P, 2, SEQ]),
                                    ALU.mult).then_inc(cos_done[kind], 1)

        def rotate(kind, count):
            nc.vector.wait_ge(sin_done[kind], count)
            nc.vector.wait_ge(cos_done[kind], count)
            dst = k_full[:, :] if kind == K else cosx[:, BUF[kind], :]
            nc.vector.tensor_tensor(dst, cosx[:, BUF[kind], :], rot[:, BUF[kind], :], ALU.add)\
                .then_inc(sum_done[kind], 1)

        def q_low(kind, count):
            nc.vector.wait_ge(qhi_done[kind], count)
            h = kind - H0
            nc.vector.tensor_tensor(q_lo[:, h, :], cosx[:, BUF[kind], :], q_hi[:, h, :].bitcast(F32), ALU.subtract)\
                .then_inc(q_ready[kind], 1)

        def k_low(b, count):
            nc.vector.wait_ge((qhi_done[K], khi1_done)[b], count)
            s = slice(SEQ * b, SEQ * (b + 1))
            nc.vector.tensor_tensor(k_lo[:, s], k_full[:, s], k_hi[:, s].bitcast(F32), ALU.subtract)\
                .then_inc((q_ready[K], k1_ready)[b], 1)

        def v_low(b, count):
            nc.vector.wait_ge(vhi_done[b], count)
            nc.vector.tensor_tensor(v_lo[:, 2 * b:2 * b + 2, :], bank_a[:, 0:SEQ].rearrange("p (k d) -> p k d", k=2),
                                    v_hi[:, 2 * b:2 * b + 2, :].bitcast(F32), ALU.subtract).then_inc(v_ready[b], 1)

        def attn_low(n, j):
            i = (j - 1) % 4
            nc.vector.wait_ge(attnhi_done, n)
            s = (slice(None), slice(2 * (i % 2), 2 * (i % 2) + 2), slice(SEQ * (i // 2), SEQ * (i // 2 + 1)))
            nc.vector.tensor_tensor(attn_lo[s], pv_ps[:, :].rearrange("p (h q) -> p h q", h=2),
                                    attn_hi[s].bitcast(F32), ALU.subtract).then_inc(attn_ready, 1)

        def add_tile(at, tile, final=None):
            dve = nc.vector
            y = y_sum[:, tile, :]
            dve.wait_ge(o_done, at(-2))
            nc.vector.tensor_tensor(y, o_ps[:, :], y, ALU.add).then_inc(y_added, 1)
            if final is None:
                return
            dve.wait_ge(y_added, at(-2))
            dve.wait_ge(xg_in, value(dve, 32 * (final + 1)))
            nc.vector.tensor_tensor(y, y, raw[:, 1, :], ALU.mult).then_inc(y_gated, 1)
            dve.wait_ge(y_gated, value(dve, final + 1))
            nc.vector.tensor_tensor(y, y, raw[:, 0, :], ALU.add).then_inc(y_final, 1)

        def dve_unit(u, final_from=4):
            dve = nc.vector
            first, last = is_unit(u, 0), is_unit(u, LAST)
            c0, c1, c2 = units(dve, u)
            n4 = slots(dve, u)
            tiles = [value(dve, (4 * u + (j + TILES - 3)) % TILES) for j in range(4)]
            for j in range(4):
                n = n4[j]
                dve.wait_ge(scores_done, n4[j + 1])
                if not (first and j == 0):
                    dve.wait_ge(pT_ps, n)
                nc.vector.tensor_tensor(probs[:, :, 0:P], s_ps[:, :, 0:P],
                                        tab[:, T_RATIO:T_RATIO + P].unsqueeze(1).to_broadcast([P, 2, P]),
                                        ALU.mult).then_inc(ratio_done, 1)
                for qt in (1, 0):
                    if qt == 0:
                        dve.wait_ge(tables_in, 16)
                        dve.wait_ge(ratio_done, n4[j + 1])
                    for h in range(2):
                        s = slice(P * qt, P * qt + P * (qt + 1))
                        i = 2 * h + qt
                        ins = nc.vector.tensor_tensor_reduce(
                            out=probs[:, h, s], in0=(probs, s_ps)[qt][:, h, s],
                            in1=tab[:, T_MASK + P * (1 - qt):T_MASK + SEQ], scale=1.0, scalar=MASKED,
                            op0=ALU.add, op1=ALU.min, accum_out=row_min[:, i:i + 1])
                ins.then_inc(masked_done, 1)
                dve.wait_ge(exp_done, n4[j + 1])
                nc.vector.reciprocal(row_inv[:, :], row_sum[:, :]).then_inc(inv_done, 1)
                dve.wait_ge(inv_done, n4[j + 1])
                for h in range(2):
                    for qt in range(2):
                        s = probs[:, h, P * qt:P * qt + P * (qt + 1)]
                        i = 2 * h + qt
                        ins = nc.vector.tensor_scalar(s, s, row_inv[:, i:i + 1], None, ALU.mult)
                ins.then_inc(probs_ready, 1)
                if j == 0:
                    cos_product(H3, bank_a, c1)
                    rotate(H3, c1)
                    q_low(H3, c1)
                elif j == 1:
                    v_low(0, c1)
                    if not last:
                        cos_product(K, bank_b, c2)
                        rotate(K, c2)
                        k_low(0, c2)
                elif j == 2:
                    v_low(1, c1)
                    if not last:
                        cos_product(H0, bank_b, c2)
                        rotate(H0, c2)
                        q_low(H0, c2)
                elif not last:
                    k_low(1, c2)
                    cos_product(H1, bank_a, c2)
                    rotate(H1, c2)
                    q_low(H1, c2)
                    cos_product(H2, bank_b, c2)
                    rotate(H2, c2)
                    q_low(H2, c2)
                if not (first and j < 3):
                    add_tile(lambda c: n4[j + c], tiles[j], n4[j] - 3 - 4 * FINAL if j >= final_from else None)
                if not (first and j == 0):
                    attn_low(n, j)
                dve.wait_ge(pThi_done, n4[j + 1])
                nc.vector.tensor_tensor(pT_lo[:, :, :], t_ps[:, :, 0:ROWS], pT_hi[:, :, :].bitcast(F32),
                                        ALU.subtract).then_inc(pT_ready, 1)

        @block.vector
        def _(dve):
            for t in range(TILES):
                if t % BLOCK_TILES == 0:
                    dve.wait_ge(x_in[t // BLOCK_TILES], 16)
                nc.vector.bn_stats(stats[:, t, :], y_sum[:, t, :]).then_inc(stat_done, 1)
                dve.wait_ge(stat_done, t + 1)
                nc.vector.bn_aggr(meanvar[:, t, :], stats[:, t, :]).then_inc(aggr_done, 1)
                if t % BLOCK_TILES == BLOCK_TILES - 1:
                    s = slice(t + 1 - BLOCK_TILES, t + 1)
                    dve.wait_ge(aggr_done, t + 1)
                    nc.vector.tensor_scalar(meanvar[:, s, 1], meanvar[:, s, 1], EPS, None, ALU.add)\
                        .then_inc(vareps_done, 1)
                    if t >= BLOCK_TILES:
                        normalise(t // BLOCK_TILES - 1)
            normalise(BLOCKS - 1)
            dve.wait_ge(ffn_in, 32)
            nc.vector.tensor_copy(ar_hi[:, :, :], ar_raw[:, :, :]).then_inc(arhi_done, 1)
            dve.wait_ge(arhi_done, 1)
            nc.vector.tensor_tensor(ar_lo[:, :, :], ar_raw[:, :, :], ar_hi[:, :, :].bitcast(F32), ALU.subtract)\
                .then_inc(ar_done, 1)
            for b in range(BLOCKS):
                dve.wait_ge(mid_ps, b + 1)
                nc.vector.tensor_copy(mid[:, BLOCK_TILES * b:BLOCK_TILES * (b + 1), :],
                                      t_ps[:, b % 2, 0:BLOCK_TILES * AR].rearrange("p (t r) -> p t r", r=AR))\
                    .then_inc(mid_done, 1)
            dve.wait_ge(mid_done, BLOCKS)
            route(dve)
            for t in range(TILES):
                dve.wait_ge(tanh_done, t + 1)
                nc.vector.scalar_tensor_tensor(out=silu[:, t % 2, :], in0=silu[:, t % 2, :], scalar=1.0,
                                               in1=(bank_a, bank_b)[t % 2][:, :], op0=ALU.add, op1=ALU.mult)\
                    .then_inc(silu_done, 1)
            cos_product(K, bank_b, 1)
            rotate(K, 1)
            cos_product(H0, bank_b, 1)
            k_low(0, 1)
            rotate(H0, 1)
            q_low(H0, 1)
            cos_product(H1, bank_a, 1)
            rotate(H1, 1)
            q_low(H1, 1)
            cos_product(H2, bank_b, 1)
            rotate(H2, 1)
            q_low(H2, 1)
            k_low(1, 1)
            dve.wait_ge(y_zero, 1)
            dve_unit(0)
            with dve.Fori(1, FINAL) as u:
                dve_unit(u)
            dve_unit(FINAL, final_from=3)
            with dve.Fori(FINAL + 1, LAST) as u:
                dve_unit(u, final_from=0)
            dve_unit(LAST, final_from=0)
            for n in range(4 * UNITS, 4 * UNITS + 3):
                if n == 4 * UNITS:
                    attn_low(n, 0)
                add_tile(lambda c: n + c, (n - 3) % TILES, n - 3 - 4 * FINAL)


def kernel(**inputs):
    import concourse.bacc as bacc
    from concourse.bass_utils import run_bass_kernel_spmd

    f32 = np.float32
    x = np.ascontiguousarray(inputs["L0_attn_hidden_states"]).reshape(TOKENS, DM)
    turn = lambda w: np.asarray(w).reshape(KV_HEADS, -1, HD, DC, P).transpose(0, 1, 4, 3, 2).reshape(KV_HEADS, -1, P, 512)
    wo = np.asarray(inputs["L0_attn_wo"]).T.reshape(KV_HEADS, GROUP, HD, DM)
    w_seq = np.ascontiguousarray(np.concatenate(
        [turn(inputs["L0_attn_wk"]), turn(inputs["L0_attn_wq"]), turn(inputs["L0_attn_wv"]), wo], axis=1)
        .reshape(KV_HEADS * CHUNKS, P, 512))
    ar = np.concatenate([np.asarray(inputs["L0_ffn_A"]).reshape(EXPERTS * RANK, DM),
                         np.asarray(inputs["L0_ffn_router_w"])], axis=0)
    a_r = np.ascontiguousarray(ar.reshape(AR, DC, P).transpose(2, 1, 0))
    b_t = np.ascontiguousarray(np.asarray(inputs["L0_ffn_B"]).transpose(0, 2, 1).reshape(EXPERTS * RANK, DM))

    inv_freq = (f32(1.0) / f32(ROPE_BASE) ** (np.arange(0, HD, 2, dtype=f32) / f32(HD))).astype(f32)
    pos = np.arange(SEQ)
    angle = np.concatenate([inv_freq, inv_freq])[:, None] * pos.astype(f32)[None, :]
    cos, sin = np.cos(angle).astype(f32), np.sin(angle).astype(f32)
    sin[:HD // 2] *= -1
    key_scale = np.where(pos < SYS_LEN, SUPPRESS, np.where(pos < SYS_LEN + IMG_LEN, ENHANCE, 1.0))
    fold = -key_scale / np.sqrt(HD)
    row, col = np.arange(P)[:, None], np.arange(P)[None, :]
    mask = np.concatenate([np.zeros((P, P)), np.where(col > row, MASKED, 0.0)], axis=1)
    ratio = np.where(row >= SYS_LEN + IMG_LEN, 1.0, 1.0 / key_scale[:P][None, :])
    tables = np.concatenate([cos, sin, cos * fold, sin * fold, mask, ratio, np.eye(P)], axis=1).astype(f32)

    arrays = {"x": x, "w_seq": w_seq, "a_r": a_r, "b_t": b_t, "tables": np.ascontiguousarray(tables)}
    nc = bacc.Bacc("TRN2", target_bir_lowering=False, num_devices=1)
    args = [nc.dram_tensor(name, a.shape, mybir.dt.from_np(a.dtype), kind="ExternalInput").ap()
            for name, a in arrays.items()]
    out = nc.dram_tensor("out", (TOKENS, DM), F32, kind="ExternalOutput").ap()
    build(nc, *args, out)
    r = run_bass_kernel_spmd(nc, [arrays], core_ids=[0])
    return r.results[0]["out"].reshape(BATCHES, SEQ, DM)
```

```python
from contextlib import ExitStack

import numpy as np

import concourse.bass as bass
from concourse import mybir

F32 = mybir.dt.float32
F32R = mybir.dt.float32r
ALU = mybir.AluOpType
ACT = mybir.ActivationFunctionType
AX = mybir.AxisListType

P = 128
BATCHES, SEQ, DM = 8, 256, 512
HEADS, KV_HEADS, HD = 32, 8, 128
GROUP = HEADS // KV_HEADS
EXPERTS, RANK = 4, 16
LORA_SCALE = 16.0 / 16.0 ** 0.5
SYS_LEN, IMG_LEN, ENHANCE, SUPPRESS = 35, 72, 1.5, 0.5
ROPE_BASE = 10000.0
EPS = 1e-5

TOKENS = BATCHES * SEQ
TILES = TOKENS // P
BLOCK = 2 * SEQ
BLOCKS = TOKENS // BLOCK
BLOCK_TILES = BLOCK // P
UNITS = KV_HEADS * BLOCKS
ITEMS = 4 * UNITS
DC = DM // P
ROWS = P + SEQ
MASKED = 3.0e38

WK, WQ, WV, WO = 0, 1, 5, 6
CHUNKS = 10
AR = EXPERTS * RANK + EXPERTS

T_COSQ, T_SINQ, T_COSK, T_SINK, T_MASK, T_RATIO, T_IDENT = 0, 256, 512, 768, 1024, 1280, 1408
T_COLS = 1536

K, H0, H1, H2, H3 = range(5)
KINDS = ["k", "h0", "h1", "h2", "h3"]
BUF = {K: 0, H0: 1, H1: 0, H2: 1, H3: 1}
V, VT0, VT1 = 5, 6, 7


def build(nc, x, w_seq, a_r, b_t, tables, out):
    g_dram = nc.dram_tensor("gate_scratch", (TILES, P, DM), F32).ap()
    x_t = x.rearrange("(t p) d -> t p d", p=P)
    out_t = out.rearrange("(t p) d -> t p d", p=P)

    ctx = ExitStack()
    with ctx:
        def sb(name, shape, dt=F32, scope=ctx):
            return scope.enter_context(nc.sbuf_tensor(name, shape, dt))

        def pb(name, shape):
            return ctx.enter_context(nc.psum_tensor(name, shape, F32))

        def sem(name):
            return ctx.enter_context(nc.semaphore(name))

        xT_hi = sb("xT_hi", [P, DC, TOKENS], F32R)
        xT_lo = sb("xT_lo", [P, DC, TOKENS], F32R)
        x_scope, ffn_scope = ExitStack(), ExitStack()
        x_sb = sb("x_sb", [P, TILES, DM], F32, x_scope)
        x_scope.close()
        ffn_bytes = 4 * (3 * DC * AR + BLOCK + 16 * TILES + TILES * AR + BLOCK + 3 * DM)
        AR_END = TILES * DM - ffn_bytes // 4 + DC * AR
        sb("ffn_pad", [P, TILES * DM - ffn_bytes // 4], F32, ffn_scope)
        ar_raw = sb("ar_raw", [P, DC, AR], F32, ffn_scope)
        ar_hi = sb("ar_hi", [P, DC, AR], F32R, ffn_scope)
        ar_lo = sb("ar_lo", [P, DC, AR], F32R, ffn_scope)
        mid_T = sb("mid_T", [AR, BLOCK], F32, ffn_scope)
        beats = sb("beats", [P, 6, TILES], F32, ffn_scope)
        keep = sb("keep", [P, TILES, EXPERTS], F32, ffn_scope)
        gate = sb("gate", [P, TILES, EXPERTS], F32, ffn_scope)
        gmax = sb("gmax", [P, TILES], F32, ffn_scope)
        gsum = sb("gsum", [P, TILES], F32, ffn_scope)
        mid = sb("mid", [P, TILES, AR], F32, ffn_scope)
        bT = sb("bT", [EXPERTS * RANK, DM], F32, ffn_scope)
        gm_T = sb("gm_T", [EXPERTS * RANK, BLOCK], F32, ffn_scope)
        silu = sb("silu", [P, 2, DM], F32, ffn_scope)
        ffn_scope.close()
        y_sum = sb("y_sum", [P, TILES, DM])
        w_hi = sb("w_hi", [P, CHUNKS, 512], F32R)
        w_lo = sb("w_lo", [P, CHUNKS, 512], F32R)
        q_hi = sb("q_hi", [P, GROUP, BLOCK], F32R)
        q_lo = sb("q_lo", [P, GROUP, BLOCK], F32R)
        k_parts = sb("k_parts", [P, 2, BLOCK], F32R)
        k_hi, k_lo = k_parts[:, 0, :], k_parts[:, 1, :]
        v_hi = sb("v_hi", [P, BLOCK_TILES, HD], F32R)
        v_lo = sb("v_lo", [P, BLOCK_TILES, HD], F32R)
        probs = sb("probs", [P, 2, ROWS])
        rot = sb("rot", [P, 2, BLOCK])
        cosx = sb("cosx", [P, 2, BLOCK])
        k_full = sb("k_full", [P, BLOCK])
        v_T = sb("v_T", [P, BLOCK])
        tab = sb("tab", [P, T_COLS])
        raw = sb("raw", [P, 2, 512])
        row_min = sb("row_min", [P, 4])
        row_sum = sb("row_sum", [P, 4])
        row_inv = sb("row_inv", [P, 4])
        zero = sb("zero", [P, 1])
        stats = sb("stats", [P, BLOCK_TILES, 6])
        meanvar = sb("meanvar", [P, TILES, 2])
        rstd = sb("rstd", [P, TILES])
        minus_half = sb("minus_half", [P, TILES])
        attn_hi = sb("attn_hi", [P, GROUP, BLOCK], F32R)
        attn_lo = sb("attn_lo", [P, GROUP, BLOCK], F32R)
        pT_hi = sb("pT_hi", [P, 2, ROWS], F32R)
        pT_lo = sb("pT_lo", [P, 2, ROWS], F32R)

        ident = tab[:, T_IDENT:T_IDENT + P]

        bank_a = pb("bank_a", [P, 512])
        bank_b = pb("bank_b", [P, 512])
        s_ps = pb("s_ps", [P, 2, 512])
        t_ps = pb("t_ps", [P, 2, 512])
        pv_ps = pb("pv_ps", [P, 512])
        o_ps = pb("o_ps", [P, 512])

        first_banks = [t_ps[:, 0, :], t_ps[:, 1, :], pv_ps[:, :], o_ps[:, :]]

        tables_in = sem("tables_in")
        x_in = [sem(f"x_in{b}") for b in range(BLOCKS)]
        ar_in = sem("ar_in")
        bT_in = sem("bT_in")
        stat_done = sem("stat_done")
        aggr_done = sem("aggr_done")
        vareps_done = sem("vareps_done")
        half_done = sem("half_done")
        rstd_done = sem("rstd_done")
        norm_done = sem("norm_done")
        xpose_done = sem("xpose_done")
        xhi_done = sem("xhi_done")
        xlo_done = sem("xlo_done")
        arhi_done = sem("arhi_done")
        ar_done = sem("ar_done")
        gate_step = sem("gate_step")
        gate_shift = sem("gate_shift")
        gate_exp = sem("gate_exp")
        gm_done = sem("gm_done")
        side_ps = sem("side_ps")
        side_out = sem("side_out")
        tanh_done = sem("tanh_done")
        gate_out = [sem(f"gate_out{i}") for i in range(2)]
        raw_in = [sem(f"raw_in{i}") for i in range(2)]
        whi_done = sem("whi_done")
        zero_done = sem("zero_done")
        w_ready = [sem(f"w_ready{c}") for c in range(CHUNKS)]
        proj_done = [sem(f"proj_done_{k}") for k in KINDS + ["v", "vt0", "vt1"]]
        rot_done = [sem(f"rot_done_{k}") for k in KINDS]
        sin_done = [sem(f"sin_done_{k}") for k in KINDS]
        cos_done = [sem(f"cos_done_{k}") for k in KINDS]
        sum_done = [sem(f"sum_done_{k}") for k in KINDS]
        qhi_done = [sem(f"qhi_done_{k}") for k in KINDS]
        q_ready = [sem(f"q_ready_{k}") for k in KINDS]
        khi1_done = sem("khi1_done")
        k1_ready = sem("k1_ready")
        vT_done = sem("vT_done")
        vhi_done = [sem(f"vhi_done{b}") for b in range(2)]
        v_ready = [sem(f"v_ready{b}") for b in range(2)]
        scores_done = sem("scores_done")
        hilo_done = sem("hilo_done")
        early_done = sem("early_done")
        ratio_done = sem("ratio_done")
        masked_done = sem("masked_done")
        exp_done = sem("exp_done")
        inv_done = sem("inv_done")
        probs_ready = sem("probs_ready")
        pT_ps = sem("pT_ps")
        pThi_done = sem("pThi_done")
        pT_ready = sem("pT_ready")
        pv_done = sem("pv_done")
        attnhi_done = sem("attnhi_done")
        attn_ready = sem("attn_ready")
        o_done = sem("o_done")
        y_added = sem("y_added")
        y_cleared = sem("y_cleared")
        xg_in = sem("xg_in")
        y_gated = sem("y_gated")
        y_final = sem("y_final")
        out_done = sem("out_done")

        steps = [("x", t) for t in range(BLOCK_TILES, TILES)]
        places = [(0, j, p) for j in range(3) for p in range(4)]
        for b in range(BLOCKS):
            steps += [("ar", b), ("mt", b)]
        steps.append(("route", 0))
        for b in range(BLOCKS):
            steps += [("gt", b)] + [("d", BLOCK_TILES * b + t) for t in range(BLOCK_TILES)]
        places += [(0, 3, p) for p in range(3)]
        for u in range(1, BLOCKS):
            places += [(u, j, p) for j in range(4) for p in ((0, 1, 2), (0, 2), (1, 2), (0, 1, 2))[j]]
        side_plan, through_ps = {}, 0
        for place, (what, i) in zip(places, steps):
            side_plan[place] = (what, i, through_ps)
            through_ps += what != "route"
        assert len(places) >= len(steps)

        SIDE_X = TILES - BLOCK_TILES

        def side_uses(u, j, p):
            return sum(1 for at, (what, _, _) in side_plan.items() if at < (u, j, p) and what != "route")

        def wait_side(eng, uses):
            if uses > SIDE_X:
                eng.wait_ge(side_out, uses - SIDE_X)
            elif uses:
                eng.wait_ge(xlo_done, BLOCK_TILES + uses)

        silu_at = {i: before + 1 - SIDE_X for what, i, before in side_plan.values() if what == "d"}

        def side_at(u, j, p):
            return side_plan.get((u, j, p)) if isinstance(u, int) else None

        block = ctx.enter_context(nc.Block())
        FINAL = UNITS - BLOCKS
        LAST = UNITS - 1

        def slots(eng, u):
            return {c: (4 * u + c if isinstance(u, int) else eng.snap(4 * u + c)) for c in range(-4, 6)}

        def units(eng, u):
            return [u + c if isinstance(u, int) or c == 0 else eng.snap(u + c) for c in range(3)]

        def is_unit(u, n):
            return isinstance(u, int) and u == n

        def value(eng, v):
            return v if isinstance(v, int) else eng.snap(v)

        @block.sync
        def _(sp):
            for b in range(BLOCKS):
                sp.dma_start(x_sb[:, BLOCK_TILES * b:BLOCK_TILES * (b + 1), :],
                             x_t[BLOCK_TILES * b:BLOCK_TILES * (b + 1), :, :].rearrange("t p d -> p t d"))\
                  .then_inc(x_in[b], 16)
                if b == 0:
                    for c in range(2):
                        sp.dma_start(raw[:, c, :], w_seq[c, :, :]).then_inc(raw_in[c], 16)
            for c in range(2, WO + 2):
                sp.wait_ge(w_ready[c - 2], 1)
                sp.dma_start(raw[:, c % 2, :], w_seq[c, :, :]).then_inc(raw_in[c % 2], 16)
            sp.wait_ge(xpose_done, -(-AR_END // DM))
            sp.dma_start(ar_raw[:, :, :], a_r).then_inc(ar_in, 16)
            sp.wait_ge(xpose_done, TILES)
            sp.dma_start(bT[:, :], b_t).then_inc(bT_in, 16)

            def load_chunk(g, c):
                before = (c - 2) % CHUNKS
                sp.wait_ge(w_ready[before], value(sp, g + 1 if c >= 2 else g))
                sp.dma_start(raw[:, c % 2, :], w_seq[value(sp, g * CHUNKS + c), :, :]).then_inc(raw_in[c % 2], 16)

            with sp.Fori(0, KV_HEADS - 1) as g:
                for c in range(WO + 2, CHUNKS):
                    load_chunk(g, c)
                g_next = sp.snap(g + 1)
                for c in range(WO + 2):
                    load_chunk(g_next, c)
            for c in range(WO + 2, CHUNKS):
                load_chunk(KV_HEADS - 1, c)
            for r in range(2):
                sp.wait_ge(gate_out[r], 16 * TILES // 2)
            for c in range(CHUNKS - 2, CHUNKS):
                sp.wait_ge(w_ready[c], KV_HEADS)
            with sp.Fori(0, TILES) as t:
                sp.dma_start(raw[:, 0, :], x_t[t, :, :]).then_inc(xg_in, 16)
                sp.dma_start(raw[:, 1, :], g_dram[t, :, :]).then_inc(xg_in, 16)
                sp.wait_ge(y_final, value(sp, t + 1))
                sp.dma_start(out_t[t, :, :], y_sum[:, t, :]).then_inc(out_done, 16)
            sp.wait_ge(out_done, 16 * TILES)

        @block.gpsimd
        def _(pool):
            nc.gpsimd.memset(minus_half[:, :], -0.5).then_inc(half_done, 1)
            nc.gpsimd.memset(zero[:, :], 0.0).then_inc(zero_done, 1)
            pool.wait_ge(half_done, 1)
            pool.wait_ge(zero_done, 1)

            def inverse_std(b):
                s = slice(BLOCK_TILES * b, BLOCK_TILES * (b + 1))
                pool.wait_ge(vareps_done, b + 1)
                nc.gpsimd.tensor_tensor(rstd[:, s], meanvar[:, s, 1], minus_half[:, s], ALU.pow).then_inc(rstd_done, 1)

            def split(g, c):
                r = c % 2
                pool.wait_ge(raw_in[r], value(pool, 16 * (CHUNKS // 2 * g + c // 2 + 1)))
                nc.gpsimd.tensor_tensor(w_hi[:, c, :], raw[:, r, :], zero[:, 0:1].to_broadcast([P, 512]),
                                        ALU.add).then_inc(whi_done, 1)
                pool.wait_ge(whi_done, value(pool, CHUNKS * g + c + 1))
                nc.gpsimd.tensor_tensor(w_lo[:, c, :], raw[:, r, :], w_hi[:, c, :].bitcast(F32),
                                        ALU.subtract).then_inc(w_ready[c], 1)

            def sin_product(kind, count):
                s = T_SINK if kind == K else T_SINQ
                v = rot[:, BUF[kind], :].rearrange("p (b t) -> p b t", b=2)
                pool.wait_ge(rot_done[kind], count)
                nc.gpsimd.tensor_tensor(v, v, tab[:, s:s + SEQ].unsqueeze(1).to_broadcast([P, 2, SEQ]),
                                        ALU.mult).then_inc(sin_done[kind], 1)

            pool.wait_ge(tables_in, 16)
            inverse_std(0)
            split(0, WK)
            split(0, WQ)
            inverse_std(1)
            split(0, WQ + 1)
            sin_product(K, 1)
            split(0, WQ + 2)
            sin_product(H0, 1)
            split(0, WQ + 3)
            sin_product(H1, 1)
            split(0, WV)
            sin_product(H2, 1)
            inverse_std(2)
            inverse_std(3)

            def group(g, g_next):
                u0 = value(pool, 4 * g)
                for i in range(BLOCKS):
                    last = g_next is None and i == BLOCKS - 1
                    own = value(pool, u0 + i + 1)
                    ahead = None if last else value(pool, u0 + i + 2)
                    for j in range(4):
                        if j == 0:
                            sin_product(H3, own)
                        if i == 0 and j == 2:
                            pool.wait_ge(proj_done[VT1], own)
                            split(g, WO)
                            split(g, WO + 1)
                        if j > 0 and not last:
                            sin_product((K, H0)[j - 1] if j < 3 else H1, ahead)
                        if i == 0 and j == 2:
                            split(g, WO + 2)
                            split(g, WO + 3)
                        if j == 3 and not last:
                            sin_product(H2, ahead)
                        if g_next is None:
                            continue
                        used = value(pool, 4 * g + 4) if (i, j) in ((2, 2), (2, 3), (3, 0), (3, 1), (3, 2)) else None
                        if (i, j) == (2, 2):
                            pool.wait_ge(proj_done[K], used)
                            split(g_next, WK)
                        elif (i, j) in ((2, 3), (3, 0), (3, 1)):
                            h = {(2, 3): 0, (3, 0): 1, (3, 1): 2}[i, j]
                            pool.wait_ge(proj_done[H0 + h], used)
                            split(g_next, WQ + h)
                        elif (i, j) == (3, 2):
                            pool.wait_ge(proj_done[H3], used)
                            split(g_next, WQ + 3)
                            pool.wait_ge(proj_done[V], used)
                            split(g_next, WV)

            with pool.Fori(0, KV_HEADS - 1) as g:
                group(g, pool.snap(g + 1))
            group(KV_HEADS - 1, None)

        def three_pass(dst, w, x0):
            for c in range(DC):
                for n, (a, x) in enumerate(((0, xT_hi), (0, xT_lo), (1, xT_hi))):
                    mm = nc.tensor.matmul(dst, w(a, c), x[:, c, bass.ds(x0, BLOCK)], start=(c == 0 and n == 0),
                                          stop=(c == DC - 1 and n == 2))
            return mm

        def turn_x(t, bank):
            nc.tensor.wait_ge(norm_done, t + 1)
            for c in range(DC):
                mm = nc.tensor.transpose(bank[:, c * P:(c + 1) * P], x_sb[:, t, c * P:(c + 1) * P], ident)
            return mm.then_inc(xpose_done, 1)

        def pe_side(u, j, p):
            side = side_at(u, j, p)
            if side is None:
                return
            pe = nc.tensor
            what, i, before = side
            if what == "route":
                return
            tiles = max(0, 4 * u + j - 3 + (p > 1 or j == 2))
            if tiles:
                pe.wait_ge(y_added, tiles)
            wait_side(pe, before)
            t0 = BLOCK_TILES * i
            if what == "x":
                pe.wait_ge(norm_done, i + 1)
                for c in range(DC):
                    mm = nc.tensor.transpose(o_ps[:, c * P:(c + 1) * P], x_sb[:, i, c * P:(c + 1) * P], ident)
                mm.then_inc(xpose_done, 1)
            elif what == "ar":
                if i == 0:
                    pe.wait_ge(ar_done, 1)
                    pe.wait_ge(xlo_done, TILES)
                three_pass(o_ps[0:AR, :], lambda w, c: (ar_hi, ar_lo)[w][:, c, :], BLOCK * i).then_inc(side_ps, 1)
            elif what == "mt":
                for t in range(BLOCK_TILES):
                    mm = nc.tensor.transpose(o_ps[:, AR * t:AR * (t + 1)], mid_T[:, t * P:(t + 1) * P],
                                             ident[0:AR, 0:AR])
                mm.then_inc(side_ps, 1)
            elif what == "gt":
                if i == 0:
                    pe.wait_ge(gm_done, 1)
                    pe.wait_ge(bT_in, 16)
                for t in range(BLOCK_TILES):
                    mm = nc.tensor.transpose(o_ps[0:EXPERTS * RANK, t * P:(t + 1) * P],
                                             mid[:, t0 + t, 0:EXPERTS * RANK], ident)
                mm.then_inc(side_ps, 1)
            else:
                t = i % BLOCK_TILES
                nc.tensor.matmul(o_ps[:, :], gm_T[:, t * P:(t + 1) * P], bT[:, :], start=True, stop=True)\
                    .then_inc(side_ps, 1)

        def project(kind, bank, chunk, x0, weights):
            nc.tensor.wait_ge(w_ready[chunk], weights)
            three_pass(bank[:, :], lambda w, c: (w_hi, w_lo)[w][:, chunk, c * P:(c + 1) * P], x0)\
                .then_inc(proj_done[kind], 1)

        def scores(b, hp):
            k0, k1 = slice(SEQ * b, SEQ * b + P), slice(SEQ * b, SEQ * b + SEQ)
            for h in range(2):
                head = 2 * hp + h
                nc.tensor.matmul(s_ps[:, h, 0:2 * P].rearrange("p (s k) -> p s k", s=2), q_hi[:, head, k0],
                                 k_parts[:, :, k0], start=True, stop=False)
                nc.tensor.matmul(s_ps[:, h, 0:P], q_lo[:, head, k0], k_hi[:, k0], start=False, stop=True)
                late = slice(SEQ * b + P, SEQ * b + SEQ)
                for n, (a, k) in enumerate(((q_hi, k_hi), (q_hi, k_lo), (q_lo, k_hi))):
                    mm = nc.tensor.matmul(s_ps[:, h, 2 * P:], a[:, head, late], k[:, k1], start=(n == 0), stop=(n == 2))
            mm.then_inc(scores_done, 1)

        def prob_value(at, j, v_count, first_items=False):
            pe = nc.tensor
            b = ((j - 1) % 4) // 2
            pe.wait_ge(pT_ready, at(0))
            pe.wait_ge(v_ready[b], v_count)
            if not first_items:
                pe.wait_ge(attn_ready, at(-1))
            full = pv_ps[:, :].rearrange("p (h q) -> p h q", h=2)
            steps = [(full, v_hi, 0, pT_hi, 0), (full[:, :, P:], v_hi, 1, pT_hi, SEQ), (full[:, :, P:], v_hi, 1, pT_lo, SEQ),
                     (full[:, :, P:], v_lo, 1, pT_hi, SEQ), (full, v_hi, 0, pT_lo, 0), (full, v_lo, 0, pT_hi, 0)]
            for i, (dst, v, kb, p, c) in enumerate(steps):
                mm = nc.tensor.matmul(dst, v[:, 2 * b + kb, :], p[:, :, c:c + (P if kb else SEQ)], start=(i == 0), stop=(i == 5))
            mm.then_inc(pv_done, 1)

        def output_tile(at, j, first_tile=False):
            pe = nc.tensor
            b, t = ((j - 3) % 4) // 2, ((j - 3) % 4) % 2
            pe.wait_ge(attn_ready, at(-1 if t == 0 else -2))
            if not first_tile:
                pe.wait_ge(y_added, at(-3))
            rows = slice(SEQ * b + P * t, SEQ * b + P * (t + 1))
            for h in range(GROUP):
                for i, (a, w) in enumerate(((attn_hi, w_hi), (attn_hi, w_lo), (attn_lo, w_hi))):
                    mm = nc.tensor.matmul(o_ps[:, :], a[:, h, rows], w[:, WO + h, :], start=(h == 0 and i == 0),
                                          stop=(h == GROUP - 1 and i == 2))
            mm.then_inc(o_done, 1)

        def pe_unit(u):
            pe = nc.tensor
            first, last = is_unit(u, 0), is_unit(u, LAST)
            c0, c1, c2 = units(pe, u)
            n4 = slots(pe, u)
            x_own = value(pe, (u % BLOCKS) * BLOCK)
            x_next = value(pe, ((u + 1) % BLOCKS) * BLOCK)
            w_own = value(pe, u // BLOCKS + 1)
            w_next = value(pe, (u + 1) // BLOCKS + 1)
            for j in range(4):
                n = n4[j]

                def tile_out():
                    if first and j < 3:
                        return
                    if j == 3:
                        for h in range(GROUP):
                            pe.wait_ge(w_ready[WO + h], w_own)
                    if isinstance(u, int) and u < BLOCKS:
                        wait_side(pe, side_uses(u, j, 2 if j != 2 else 0))
                    output_tile(lambda c: n4[j + c], j, first_tile=first)

                if j == 2:
                    tile_out()
                pe_side(u, j, 0)
                if j == 0:
                    pe.wait_ge(cos_done[H2], c1)
                    pe.wait_ge(cos_done[H1], c1)
                    project(H3, bank_a, WQ + 3, x_own, w_own)
                    pe_side(u, j, 1)
                    project(V, bank_b, WV, x_own, w_own)
                elif j in (1, 2):
                    pe.wait_ge(vT_done, c1)
                    if j == 1:
                        pe.wait_ge(cos_done[H3], c1)
                    else:
                        pe.wait_ge(v_ready[0], c1)
                    for kb in range(2):
                        t = 2 * (j - 1) + kb
                        mm = nc.tensor.transpose(bank_a[:, kb * P:(kb + 1) * P], v_T[:, t * P:(t + 1) * P], ident)
                    mm.then_inc(proj_done[VT0 if j == 1 else VT1], 1)
                    if not last:
                        if j == 1:
                            if isinstance(u, int) and u < BLOCKS - 1:
                                pe.wait_ge(xlo_done, BLOCK_TILES * (u + 2))
                            project(K, bank_b, WK, x_next, w_next)
                        else:
                            pe.wait_ge(cos_done[K], c2)
                            project(H0, bank_b, WQ, x_next, w_next)
                    pe_side(u, j, 1)
                elif not last:
                    pe.wait_ge(v_ready[1], c1)
                    project(H1, bank_a, WQ + 1, x_next, w_next)
                    pe_side(u, j, 1)
                    pe.wait_ge(cos_done[H0], c2)
                    project(H2, bank_b, WQ + 2, x_next, w_next)
                if j != 2:
                    tile_out()
                if not (first and j == 0):
                    prob_value(lambda c: n4[j + c], j, v_count=c1 if j > 0 else c0, first_items=first and j == 1)
                pe_side(u, j, 2)
                pe.wait_ge(probs_ready, n4[j + 1])
                if not (first and j == 0):
                    pe.wait_ge(pT_ready, n)
                for h in range(2):
                    for s in range(ROWS // P):
                        mm = nc.tensor.transpose(t_ps[:, h, s * P:(s + 1) * P], probs[:, h, s * P:(s + 1) * P], ident)
                mm.then_inc(pT_ps, 1)
                pe_side(u, j, 3)
                if not (last and j == 3):
                    pe.wait_ge(masked_done, n4[j + 1])
                    if j == 0:
                        pe.wait_ge(q_ready[H2], c1)
                        pe.wait_ge(q_ready[H3], c1)
                    elif j == 1:
                        pe.wait_ge(k1_ready, c1)
                    elif j == 3:
                        for kind in (K, H0, H1):
                            pe.wait_ge(q_ready[kind], c2)
                    scores(b=((j + 1) % 4) // 2, hp=(j + 1) % 2)

        @block.tensor
        def _(pe):
            pe.wait_ge(tables_in, 16)
            for t in range(BLOCK_TILES):
                turn_x(t, first_banks[t])
            pe.wait_ge(xlo_done, BLOCK_TILES)
            project(K, bank_b, WK, 0, 1)
            project(H0, bank_a, WQ, 0, 1)
            pe.wait_ge(cos_done[K], 1)
            project(H1, bank_b, WQ + 1, 0, 1)
            pe.wait_ge(cos_done[H0], 1)
            project(H2, bank_a, WQ + 2, 0, 1)
            for kind in (K, H0, H1):
                pe.wait_ge(q_ready[kind], 1)
            scores(0, 0)
            for u in range(BLOCKS):
                pe_unit(u)
            with pe.Fori(BLOCKS, LAST) as u:
                pe_unit(u)
            pe_unit(LAST)
            n = 4 * UNITS
            for m in range(n, n + 3):
                output_tile(lambda c: m + c, m % 4)
                if m == n:
                    prob_value(lambda c: m + c, 0, v_count=UNITS)

        def x_high(t, bank):
            nc.scalar.wait_ge(xpose_done, t + 1)
            nc.scalar.activation(xT_hi[:, :, t * P:(t + 1) * P], bank.rearrange("p (c t) -> p c t", c=DC),
                                 ACT.Copy).then_inc(xhi_done, 1)

        def store_silu(t):
            nc.scalar.wait_ge(side_out, silu_at[t])
            nc.scalar.dma_start(g_dram[t, :, :], silu[:, t % 2, :]).then_inc(gate_out[t % 2], 16)

        def act_side(u, j, p):
            side = side_at(u, j, p)
            if side is None:
                return
            act = nc.scalar
            what, i, before = side
            if what == "x":
                x_high(i, o_ps[:, :])
            elif what == "ar":
                act.wait_ge(side_ps, before + 1 - SIDE_X)
                nc.scalar.activation(mid_T[:, :], o_ps[0:AR, :], ACT.Copy).then_inc(side_out, 1)
            elif what == "route":
                act.wait_ge(gate_shift, 1)
                nc.scalar.activation(gate[:, :, :], gate[:, :, :], ACT.Exp).then_inc(gate_exp, 1)
            elif what == "gt":
                act.wait_ge(side_ps, before + 1 - SIDE_X)
                nc.scalar.activation(gm_T[:, :], o_ps[0:EXPERTS * RANK, :], ACT.Copy).then_inc(side_out, 1)
            elif what == "d":
                if i >= 1:
                    store_silu(i - 1)
                act.wait_ge(side_ps, before + 1 - SIDE_X)
                if i >= 2:
                    act.wait_ge(gate_out[i % 2], 16 * (i // 2))
                nc.scalar.activation(silu[:, i % 2, :], o_ps[:, :], ACT.Tanh).then_inc(tanh_done, 1)

        def swap_halves(kind, bank, count, before, before_count):
            act = nc.scalar
            act.wait_ge(proj_done[kind], count)
            if before is not None:
                act.wait_ge(sum_done[before], before_count)
            r = rot[:, BUF[kind], :]
            half = HD // 2
            nc.scalar.activation(r[0:half, :], bank[half:HD, :], ACT.Copy)
            nc.scalar.activation(r[half:HD, :], bank[0:half, :], ACT.Copy).then_inc(rot_done[kind], 1)

        def q_high(kind, count, used):
            act = nc.scalar
            act.wait_ge(sum_done[kind], count)
            if used is not None:
                act.wait_ge(scores_done, used)
            nc.scalar.activation(q_hi[:, kind - H0, :], cosx[:, BUF[kind], :], ACT.Copy).then_inc(qhi_done[kind], 1)

        def k_high(b, count, used):
            act = nc.scalar
            act.wait_ge(sum_done[K], count)
            if used is not None:
                act.wait_ge(scores_done, used)
            s = slice(SEQ * b, SEQ * (b + 1))
            nc.scalar.activation(k_hi[:, s], k_full[:, s], ACT.Copy).then_inc((qhi_done[K], khi1_done)[b], 1)

        def v_high(b, count, used):
            act = nc.scalar
            act.wait_ge(proj_done[VT0 + b], count)
            if used is not None:
                act.wait_ge(pv_done, used)
            nc.scalar.activation(v_hi[:, 2 * b:2 * b + 2, :], bank_a[:, 0:SEQ].rearrange("p (k d) -> p k d", k=2),
                                 ACT.Copy).then_inc(vhi_done[b], 1)

        def attn_high(n, j, old=None):
            act = nc.scalar
            i = (j - 1) % 4
            act.wait_ge(pv_done, n)
            if old is not None:
                act.wait_ge(o_done, old)
            nc.scalar.activation(attn_hi[:, 2 * (i % 2):2 * (i % 2) + 2, SEQ * (i // 2):SEQ * (i // 2 + 1)],
                                 pv_ps[:, :].rearrange("p (h q) -> p h q", h=2), ACT.Copy).then_inc(attnhi_done, 1)

        def act_unit(u):
            act = nc.scalar
            first, last = is_unit(u, 0), is_unit(u, LAST)
            c0, c1, c2 = units(act, u)
            n4 = slots(act, u)
            for j in range(4):
                n = n4[j]
                act.wait_ge(scores_done, n4[j + 1])
                if not (first and j == 0):
                    act.wait_ge(pT_ps, n)
                nc.scalar.activation(probs[:, :, 0:P], s_ps[:, :, P:2 * P], ACT.Copy).then_inc(hilo_done, 1)
                act_side(u, j, 0)
                if j == 0:
                    q_high(H2, c1, None if first else n4[0])
                    swap_halves(H3, bank_a, c1, H2, c1)
                    act_side(u, j, 1)
                elif j == 1:
                    v_high(0, c1, None if first else n4[-2])
                elif j == 2 and not last:
                    k_high(0, c2, n4[2])
                elif j == 3 and not last:
                    q_high(H0, c2, n4[3])
                    k_high(1, c2, n4[4])
                    swap_halves(H1, bank_a, c2, K, c2)
                    act_side(u, j, 1)
                act.wait_ge(masked_done, n4[j + 1])
                for h in range(2):
                    for qt in range(2):
                        s = probs[:, h, P * qt:P * qt + P * (qt + 1)]
                        i = 2 * h + qt
                        a = nc.scalar.activation(s, s, ACT.Exp, bias=row_min[:, i:i + 1], scale=-1.0,
                                                 accum_out=row_sum[:, i:i + 1])
                a.then_inc(exp_done, 1)
                if j == 0:
                    act.wait_ge(proj_done[V], c1)
                    if not first:
                        act.wait_ge(proj_done[VT1], c0)
                    nc.scalar.activation(v_T[:, :], bank_b[:, :], ACT.Copy).then_inc(vT_done, 1)
                    q_high(H3, c1, None if first else n4[0])
                elif j == 1 and not last:
                    swap_halves(K, bank_b, c2, H1, c1)
                    act_side(u, j, 1)
                elif j == 2:
                    v_high(1, c1, None if first else n4[0])
                    if not last:
                        swap_halves(H0, bank_b, c2, H3, c1)
                        act_side(u, j, 1)
                elif j == 3 and not last:
                    swap_halves(H2, bank_b, c2, H0, c2)
                    q_high(H1, c2, n4[3])
                if not (first and j == 0):
                    attn_high(n, j, None if first else n4[(-3, -2, -2, 0)[j]])
                act_side(u, j, 2)
                act.wait_ge(pT_ps, n4[j + 1])
                if not (first and j == 0):
                    act.wait_ge(pv_done, n)
                nc.scalar.activation(pT_hi[:, :, :], t_ps[:, :, 0:ROWS], ACT.Copy).then_inc(pThi_done, 1)
                act_side(u, j, 3)
                if isinstance(u, int) and (u, j) == (BLOCKS - 1, 3):
                    store_silu(TILES - 1)

        @block.scalar
        def _(act):
            nc.scalar.dma_start(tab[:, :], tables).then_inc(tables_in, 16)
            for t in range(BLOCK_TILES):
                x_high(t, first_banks[t])
            swap_halves(K, bank_b, 1, None, None)
            swap_halves(H0, bank_a, 1, None, None)
            k_high(0, 1, None)
            q_high(H0, 1, None)
            swap_halves(H1, bank_b, 1, K, 1)
            q_high(H1, 1, None)
            swap_halves(H2, bank_a, 1, H0, 1)
            k_high(1, 1, None)
            for u in range(BLOCKS):
                act_unit(u)
            with act.Fori(BLOCKS, LAST) as u:
                act_unit(u)
            act_unit(LAST)
            attn_high(4 * UNITS, 0)

        def statistics(b):
            dve = nc.vector
            dve.wait_ge(x_in[b], 16)
            s = slice(BLOCK_TILES * b, BLOCK_TILES * (b + 1))
            for i in range(BLOCK_TILES):
                ins = nc.vector.bn_stats(stats[:, i, :], x_sb[:, BLOCK_TILES * b + i, :])
            ins.then_inc(stat_done, 1)
            dve.wait_ge(stat_done, b + 1)
            for i in range(BLOCK_TILES):
                ins = nc.vector.bn_aggr(meanvar[:, BLOCK_TILES * b + i, :], stats[:, i, :])
            ins.then_inc(aggr_done, 1)
            dve.wait_ge(aggr_done, b + 1)
            nc.vector.tensor_scalar(meanvar[:, s, 1], meanvar[:, s, 1], EPS, None, ALU.add).then_inc(vareps_done, 1)

        def normalise(b):
            nc.vector.wait_ge(rstd_done, b + 1)
            for t in range(BLOCK_TILES * b, BLOCK_TILES * (b + 1)):
                nc.vector.tensor_scalar(x_sb[:, t, :], x_sb[:, t, :], meanvar[:, t, 0:1], rstd[:, t:t + 1],
                                        ALU.subtract, ALU.mult).then_inc(norm_done, 1)

        def x_low(t, bank):
            s = slice(t * P, (t + 1) * P)
            nc.vector.wait_ge(xhi_done, t + 1)
            return nc.vector.tensor_tensor(xT_lo[:, :, s], bank.rearrange("p (c t) -> p c t", c=DC),
                                           xT_hi[:, :, s].bitcast(F32), ALU.subtract).then_inc(xlo_done, 1)

        def split_ar():
            dve = nc.vector
            dve.wait_ge(ar_in, 16)
            nc.vector.tensor_copy(ar_hi[:, :, :], ar_raw[:, :, :]).then_inc(arhi_done, 1)
            dve.wait_ge(arhi_done, 1)
            nc.vector.tensor_tensor(ar_lo[:, :, :], ar_raw[:, :, :], ar_hi[:, :, :].bitcast(F32), ALU.subtract)\
                .then_inc(ar_done, 1)

        def dve_side(u, j, p):
            side = side_at(u, j, p)
            if side is None:
                return
            dve = nc.vector
            what, i, before = side
            if what == "x":
                x_low(i, o_ps[:, :])
            elif what == "mt":
                dve.wait_ge(side_ps, before + 1 - SIDE_X)
                nc.vector.tensor_copy(mid[:, BLOCK_TILES * i:BLOCK_TILES * (i + 1), :],
                                      o_ps[:, 0:BLOCK_TILES * AR].rearrange("p (t r) -> p t r", r=AR))\
                    .then_inc(side_out, 1)
            elif what == "route":
                dve.wait_ge(side_out, before - SIDE_X)
                route(dve)
            elif what == "d":
                dve.wait_ge(tanh_done, i + 1)
                nc.vector.scalar_tensor_tensor(out=silu[:, i % 2, :], in0=silu[:, i % 2, :], scalar=1.0,
                                               in1=o_ps[:, :], op0=ALU.add, op1=ALU.mult).then_inc(side_out, 1)

        def route(dve):
            steps = [0]

            def link(ins):
                steps[0] += 1
                ins.then_inc(gate_step, 1)
                dve.wait_ge(gate_step, steps[0])

            logit = lambda e: mid[:, :, EXPERTS * RANK + e]
            pairs = [(0, 1), (0, 2), (0, 3), (1, 2), (1, 3), (2, 3)]
            c = {p: beats[:, i, :] for i, p in enumerate(pairs)}
            for a, b in pairs:
                ins = nc.vector.tensor_tensor(c[a, b], logit(a), logit(b), ALU.is_ge)
            link(ins)
            tt = nc.vector.tensor_tensor
            tt(keep[:, :, 0], c[0, 1], c[0, 2], ALU.add)
            tt(keep[:, :, 1], c[1, 2], c[1, 3], ALU.add)
            tt(keep[:, :, 2], c[2, 3], c[0, 2], ALU.subtract)
            link(tt(keep[:, :, 3], c[0, 3], c[1, 3], ALU.add))
            tt(keep[:, :, 0], keep[:, :, 0], c[0, 3], ALU.add)
            tt(keep[:, :, 1], keep[:, :, 1], c[0, 1], ALU.subtract)
            tt(keep[:, :, 2], keep[:, :, 2], c[1, 2], ALU.subtract)
            link(tt(keep[:, :, 3], keep[:, :, 3], c[2, 3], ALU.add))
            ts = nc.vector.tensor_scalar
            ts(keep[:, :, 0], keep[:, :, 0], 2.0, None, ALU.is_ge)
            ts(keep[:, :, 1], keep[:, :, 1], 0.5, None, ALU.is_ge)
            ts(keep[:, :, 2], keep[:, :, 2], -0.5, None, ALU.is_ge)
            ts(keep[:, :, 3], keep[:, :, 3], 1.5, None, ALU.is_lt)
            logits = mid[:, :, EXPERTS * RANK:AR]
            link(nc.vector.tensor_reduce(gmax[:, :], logits, AX.X, ALU.max))
            wide = lambda v: v.unsqueeze(2).to_broadcast([P, TILES, EXPERTS])
            tt(gate[:, :, :], logits, wide(gmax[:, :]), ALU.subtract).then_inc(gate_shift, 1)
            dve.wait_ge(gate_exp, 1)
            link(tt(gate[:, :, :], gate[:, :, :], keep[:, :, :], ALU.mult))
            link(nc.vector.tensor_reduce(gsum[:, :], gate[:, :, :], AX.X, ALU.add))
            link(nc.vector.reciprocal(gsum[:, :], gsum[:, :]))
            link(ts(gsum[:, :], gsum[:, :], LORA_SCALE / 2, None, ALU.mult))
            link(tt(gate[:, :, :], gate[:, :, :], wide(gsum[:, :]), ALU.mult))
            for e in range(EXPERTS):
                m = mid[:, :, RANK * e:RANK * (e + 1)]
                ins = tt(m, m, gate[:, :, e].unsqueeze(2).to_broadcast([P, TILES, RANK]), ALU.mult)
            ins.then_inc(gm_done, 1)

        def cos_product(kind, bank, count, old=None, old_count=None):
            s = T_COSK if kind == K else T_COSQ
            if old is not None:
                nc.vector.wait_ge(q_ready[old], old_count)
            nc.vector.wait_ge(rot_done[kind], count)
            nc.vector.tensor_tensor(cosx[:, BUF[kind], :].rearrange("p (b t) -> p b t", b=2),
                                    bank[:, :].rearrange("p (b t) -> p b t", b=2),
                                    tab[:, s:s + SEQ].unsqueeze(1).to_broadcast([P, 2, SEQ]),
                                    ALU.mult).then_inc(cos_done[kind], 1)

        def rotate(kind, count):
            nc.vector.wait_ge(sin_done[kind], count)
            nc.vector.wait_ge(cos_done[kind], count)
            dst = k_full[:, :] if kind == K else cosx[:, BUF[kind], :]
            nc.vector.tensor_tensor(dst, cosx[:, BUF[kind], :], rot[:, BUF[kind], :], ALU.add)\
                .then_inc(sum_done[kind], 1)

        def q_low(kind, count):
            nc.vector.wait_ge(qhi_done[kind], count)
            h = kind - H0
            nc.vector.tensor_tensor(q_lo[:, h, :], cosx[:, BUF[kind], :], q_hi[:, h, :].bitcast(F32), ALU.subtract)\
                .then_inc(q_ready[kind], 1)

        def k_low(b, count):
            nc.vector.wait_ge((qhi_done[K], khi1_done)[b], count)
            s = slice(SEQ * b, SEQ * (b + 1))
            nc.vector.tensor_tensor(k_lo[:, s], k_full[:, s], k_hi[:, s].bitcast(F32), ALU.subtract)\
                .then_inc((q_ready[K], k1_ready)[b], 1)

        def v_low(b, count):
            nc.vector.wait_ge(vhi_done[b], count)
            nc.vector.tensor_tensor(v_lo[:, 2 * b:2 * b + 2, :], bank_a[:, 0:SEQ].rearrange("p (k d) -> p k d", k=2),
                                    v_hi[:, 2 * b:2 * b + 2, :].bitcast(F32), ALU.subtract).then_inc(v_ready[b], 1)

        def attn_low(n, j):
            i = (j - 1) % 4
            nc.vector.wait_ge(attnhi_done, n)
            s = (slice(None), slice(2 * (i % 2), 2 * (i % 2) + 2), slice(SEQ * (i // 2), SEQ * (i // 2 + 1)))
            nc.vector.tensor_tensor(attn_lo[s], pv_ps[:, :].rearrange("p (h q) -> p h q", h=2),
                                    attn_hi[s].bitcast(F32), ALU.subtract).then_inc(attn_ready, 1)

        def turned_low(n):
            nc.vector.wait_ge(pThi_done, n)
            nc.vector.tensor_tensor(pT_lo[:, :, :], t_ps[:, :, 0:ROWS], pT_hi[:, :, :].bitcast(F32),
                                    ALU.subtract).then_inc(pT_ready, 1)

        def add_tile(at, tile, final=None, start=False):
            dve = nc.vector
            y = y_sum[:, tile, :]
            dve.wait_ge(o_done, at(-2))
            if start:
                nc.vector.tensor_copy(y, o_ps[:, :]).then_inc(y_added, 1)
                return
            nc.vector.tensor_tensor(y, o_ps[:, :], y, ALU.add).then_inc(y_added, 1)
            if final is None:
                return
            dve.wait_ge(y_added, at(-2))
            dve.wait_ge(xg_in, value(dve, 32 * (final + 1)))
            nc.vector.tensor_tensor(y, y, raw[:, 1, :], ALU.mult).then_inc(y_gated, 1)
            dve.wait_ge(y_gated, value(dve, final + 1))
            nc.vector.tensor_tensor(y, y, raw[:, 0, :], ALU.add).then_inc(y_final, 1)

        def dve_unit(u, final_from=4):
            dve = nc.vector
            first, last = is_unit(u, 0), is_unit(u, LAST)
            c0, c1, c2 = units(dve, u)
            n4 = slots(dve, u)
            tiles = [value(dve, (4 * u + (j + TILES - 3)) % TILES) for j in range(4)]
            for j in range(4):
                n = n4[j]

                def tile_in():
                    if not (first and j < 3):
                        add_tile(lambda c: n4[j + c], tiles[j], n4[j] - 3 - 4 * FINAL if j >= final_from else None,
                                 start=isinstance(u, int) and u < BLOCKS)

                if not (first and j <= 1):
                    attn_low(n4[j - 1], j - 1)
                dve.wait_ge(hilo_done, n4[j + 1])
                early = probs[:, :, 0:P]
                nc.vector.tensor_tensor(early, s_ps[:, :, 0:P], early, ALU.add).then_inc(early_done, 1)

                def masked(h, qt):
                    s = slice(P * qt, P * qt + P * (qt + 1))
                    i = 2 * h + qt
                    return nc.vector.tensor_tensor_reduce(
                        out=probs[:, h, s], in0=(probs[:, h, 0:P], s_ps[:, h, 2 * P:])[qt],
                        in1=tab[:, T_MASK + P * (1 - qt):T_MASK + SEQ], scale=1.0, scalar=MASKED,
                        op0=ALU.add, op1=ALU.min, accum_out=row_min[:, i:i + 1])

                masked(0, 1)
                dve.wait_ge(early_done, n4[j + 1])
                nc.vector.tensor_tensor(early, early, tab[:, T_RATIO:T_RATIO + P].unsqueeze(1).to_broadcast([P, 2, P]),
                                        ALU.mult).then_inc(ratio_done, 1)
                masked(1, 1)
                dve.wait_ge(tables_in, 16)
                dve.wait_ge(ratio_done, n4[j + 1])
                masked(0, 0)
                ins = masked(1, 0)
                ins.then_inc(masked_done, 1)
                dve_side(u, j, 0)
                if j == 0:
                    q_low(H2, c1)
                elif j == 2 and not last:
                    k_low(0, c2)
                elif j == 3 and not last:
                    q_low(H0, c2)
                if not (first and j == 0):
                    turned_low(n)
                if j == 1:
                    v_low(0, c1)
                elif j == 0:
                    if first:
                        statistics(2)
                        statistics(3)
                    cos_product(H3, bank_a, c1, H2, c1)
                    dve_side(u, j, 1)
                    rotate(H3, c1)
                elif j == 3 and not last:
                    k_low(1, c2)
                    cos_product(H1, bank_a, c2)
                    dve_side(u, j, 1)
                    rotate(H1, c2)
                dve.wait_ge(exp_done, n4[j + 1])
                nc.vector.reciprocal(row_inv[:, :], row_sum[:, :]).then_inc(inv_done, 1)
                dve.wait_ge(inv_done, n4[j + 1])
                for h in range(2):
                    for qt in range(2):
                        s = probs[:, h, P * qt:P * qt + P * (qt + 1)]
                        i = 2 * h + qt
                        ins = nc.vector.tensor_scalar(s, s, row_inv[:, i:i + 1], None, ALU.mult)
                ins.then_inc(probs_ready, 1)
                if j == 0:
                    q_low(H3, c1)
                    if first:
                        normalise(2)
                elif j == 1:
                    if not last:
                        cos_product(K, bank_b, c2, H1, c1)
                        dve_side(u, j, 1)
                        rotate(K, c2)
                    if first:
                        normalise(3)
                elif j == 2:
                    tile_in()
                    v_low(1, c1)
                    if not last:
                        cos_product(H0, bank_b, c2, H3, c1)
                        dve_side(u, j, 1)
                        rotate(H0, c2)
                elif not last:
                    cos_product(H2, bank_b, c2, H0, c2)
                    q_low(H1, c2)
                    rotate(H2, c2)
                if j != 2:
                    tile_in()
                dve_side(u, j, 2)
                dve_side(u, j, 3)
                if first and j == 2:
                    split_ar()

        @block.vector
        def _(dve):
            statistics(0)
            normalise(0)
            for t in range(BLOCK_TILES):
                x_low(t, first_banks[t])
            statistics(1)
            cos_product(K, bank_b, 1)
            cos_product(H0, bank_a, 1)
            rotate(K, 1)
            k_low(0, 1)
            rotate(H0, 1)
            q_low(H0, 1)
            cos_product(H1, bank_b, 1)
            rotate(H1, 1)
            q_low(H1, 1)
            cos_product(H2, bank_a, 1)
            rotate(H2, 1)
            k_low(1, 1)
            normalise(1)
            for u in range(BLOCKS):
                dve_unit(u)
            for i in range(2):
                dve.wait_ge(gate_out[i], 16 * TILES // 2)
            nc.vector.memset(y_sum[:, TILES - 3:TILES, :], 0.0).then_inc(y_cleared, 1)
            dve.wait_ge(y_cleared, 1)
            with dve.Fori(BLOCKS, FINAL) as u:
                dve_unit(u)
            dve_unit(FINAL, final_from=3)
            with dve.Fori(FINAL + 1, LAST) as u:
                dve_unit(u, final_from=0)
            dve_unit(LAST, final_from=0)
            n = 4 * UNITS
            attn_low(n - 1, 3)
            turned_low(n)
            for n in range(n, n + 3):
                if n == 4 * UNITS:
                    attn_low(n, 0)
                add_tile(lambda c: n + c, (n - 3) % TILES, n - 3 - 4 * FINAL)


def kernel(**inputs):
    import concourse.bacc as bacc
    from concourse.bass_utils import run_bass_kernel_spmd

    f32 = np.float32
    x = np.ascontiguousarray(inputs["L0_attn_hidden_states"]).reshape(TOKENS, DM)
    turn = lambda w: np.asarray(w).reshape(KV_HEADS, -1, HD, DC, P).transpose(0, 1, 4, 3, 2).reshape(KV_HEADS, -1, P, 512)
    wo = np.asarray(inputs["L0_attn_wo"]).T.reshape(KV_HEADS, GROUP, HD, DM)
    w_seq = np.ascontiguousarray(np.concatenate(
        [turn(inputs["L0_attn_wk"]), turn(inputs["L0_attn_wq"]), turn(inputs["L0_attn_wv"]), wo], axis=1)
        .reshape(KV_HEADS * CHUNKS, P, 512))
    ar = np.concatenate([np.asarray(inputs["L0_ffn_A"]).reshape(EXPERTS * RANK, DM),
                         np.asarray(inputs["L0_ffn_router_w"])], axis=0)
    a_r = np.ascontiguousarray(ar.reshape(AR, DC, P).transpose(2, 1, 0))
    b_t = np.ascontiguousarray(np.asarray(inputs["L0_ffn_B"]).transpose(0, 2, 1).reshape(EXPERTS * RANK, DM))

    inv_freq = (f32(1.0) / f32(ROPE_BASE) ** (np.arange(0, HD, 2, dtype=f32) / f32(HD))).astype(f32)
    pos = np.arange(SEQ)
    angle = np.concatenate([inv_freq, inv_freq])[:, None] * pos.astype(f32)[None, :]
    cos, sin = np.cos(angle).astype(f32), np.sin(angle).astype(f32)
    sin[:HD // 2] *= -1
    key_scale = np.where(pos < SYS_LEN, SUPPRESS, np.where(pos < SYS_LEN + IMG_LEN, ENHANCE, 1.0))
    fold = -key_scale / np.sqrt(HD)
    row, col = np.arange(P)[:, None], np.arange(P)[None, :]
    mask = np.concatenate([np.zeros((P, P)), np.where(col > row, MASKED, 0.0)], axis=1)
    ratio = np.where(row >= SYS_LEN + IMG_LEN, 1.0, 1.0 / key_scale[:P][None, :])
    tables = np.concatenate([cos, sin, cos * fold, sin * fold, mask, ratio, np.eye(P)], axis=1).astype(f32)

    arrays = {"x": x, "w_seq": w_seq, "a_r": a_r, "b_t": b_t, "tables": np.ascontiguousarray(tables)}
    nc = bacc.Bacc("TRN2", target_bir_lowering=False, num_devices=1)
    args = [nc.dram_tensor(name, a.shape, mybir.dt.from_np(a.dtype), kind="ExternalInput").ap()
            for name, a in arrays.items()]
    out = nc.dram_tensor("out", (TOKENS, DM), F32, kind="ExternalOutput").ap()
    build(nc, *args, out)
    r = run_bass_kernel_spmd(nc, [arrays], core_ids=[0])
    return r.results[0]["out"].reshape(BATCHES, SEQ, DM)
```

```python
from contextlib import ExitStack

import numpy as np

import concourse.bass as bass
from concourse import mybir

F32 = mybir.dt.float32
F32R = mybir.dt.float32r
ALU = mybir.AluOpType
ACT = mybir.ActivationFunctionType
AX = mybir.AxisListType

P = 128
BATCHES, SEQ, DM = 8, 256, 512
HEADS, KV_HEADS, HD = 32, 8, 128
GROUP = HEADS // KV_HEADS
EXPERTS, RANK = 4, 16
LORA_SCALE = 16.0 / 16.0 ** 0.5
SYS_LEN, IMG_LEN, ENHANCE, SUPPRESS = 35, 72, 1.5, 0.5
ROPE_BASE = 10000.0
EPS = 1e-5

TOKENS = BATCHES * SEQ
TILES = TOKENS // P
BLOCK = 2 * SEQ
BLOCKS = TOKENS // BLOCK
BLOCK_TILES = BLOCK // P
UNITS = KV_HEADS * BLOCKS
ITEMS = 4 * UNITS
DC = DM // P
ROWS = P + SEQ
MASKED = 3.0e38

WK, WQ, WV, WO = 0, 1, 5, 6
CHUNKS = 10
AR = EXPERTS * RANK + EXPERTS

T_COSQ, T_SINQ, T_COSK, T_SINK, T_MASK, T_RATIO, T_IDENT = 0, 256, 512, 768, 1024, 1280, 1408
T_COLS = 1536

K, H0, H1, H2, H3 = range(5)
KINDS = ["k", "h0", "h1", "h2", "h3"]
BUF = {K: 0, H0: 1, H1: 0, H2: 1, H3: 1}
V, VT0, VT1 = 5, 6, 7


def build(nc, x, w_seq, a_r, b_t, tables, out):
    g_dram = nc.dram_tensor("gate_scratch", (TILES, P, DM), F32).ap()
    x_t = x.rearrange("(t p) d -> t p d", p=P)
    out_t = out.rearrange("(t p) d -> t p d", p=P)

    ctx = ExitStack()
    with ctx:
        def sb(name, shape, dt=F32, scope=ctx):
            return scope.enter_context(nc.sbuf_tensor(name, shape, dt))

        def pb(name, shape):
            return ctx.enter_context(nc.psum_tensor(name, shape, F32))

        def sem(name):
            return ctx.enter_context(nc.semaphore(name))

        xT_hi = sb("xT_hi", [P, DC, TOKENS], F32R)
        xT_lo = sb("xT_lo", [P, DC, TOKENS], F32R)
        x_scope, ffn_scope = ExitStack(), ExitStack()
        x_sb = sb("x_sb", [P, TILES, DM], F32, x_scope)
        x_scope.close()
        ffn_bytes = 4 * (3 * DC * AR + BLOCK + 16 * TILES + TILES * AR + BLOCK + 3 * DM)
        AR_END = TILES * DM - ffn_bytes // 4 + DC * AR
        sb("ffn_pad", [P, TILES * DM - ffn_bytes // 4], F32, ffn_scope)
        ar_raw = sb("ar_raw", [P, DC, AR], F32, ffn_scope)
        ar_hi = sb("ar_hi", [P, DC, AR], F32R, ffn_scope)
        ar_lo = sb("ar_lo", [P, DC, AR], F32R, ffn_scope)
        mid_T = sb("mid_T", [AR, BLOCK], F32, ffn_scope)
        beats = sb("beats", [P, 6, TILES], F32, ffn_scope)
        keep = sb("keep", [P, TILES, EXPERTS], F32, ffn_scope)
        gate = sb("gate", [P, TILES, EXPERTS], F32, ffn_scope)
        gmax = sb("gmax", [P, TILES], F32, ffn_scope)
        gsum = sb("gsum", [P, TILES], F32, ffn_scope)
        mid = sb("mid", [P, TILES, AR], F32, ffn_scope)
        bT = sb("bT", [EXPERTS * RANK, DM], F32, ffn_scope)
        gm_T = sb("gm_T", [EXPERTS * RANK, BLOCK], F32, ffn_scope)
        silu = sb("silu", [P, 2, DM], F32, ffn_scope)
        ffn_scope.close()
        y_sum = sb("y_sum", [P, TILES, DM])
        w_hi = sb("w_hi", [P, CHUNKS, 512], F32R)
        w_lo = sb("w_lo", [P, CHUNKS, 512], F32R)
        q_hi = sb("q_hi", [P, GROUP, BLOCK], F32R)
        q_lo = sb("q_lo", [P, GROUP, BLOCK], F32R)
        k_parts = sb("k_parts", [P, 2, BLOCK], F32R)
        k_hi, k_lo = k_parts[:, 0, :], k_parts[:, 1, :]
        v_hi = sb("v_hi", [P, BLOCK_TILES, HD], F32R)
        v_lo = sb("v_lo", [P, BLOCK_TILES, HD], F32R)
        probs = sb("probs", [P, 2, ROWS])
        rot = sb("rot", [P, 2, BLOCK])
        cosx = sb("cosx", [P, 2, BLOCK])
        k_full = sb("k_full", [P, BLOCK])
        v_T = sb("v_T", [P, BLOCK])
        tab = sb("tab", [P, T_COLS])
        raw = sb("raw", [P, 2, 512])
        row_min = sb("row_min", [P, 4])
        row_sum = sb("row_sum", [P, 4])
        row_inv = sb("row_inv", [P, 4])
        zero = sb("zero", [P, 1])
        stats = sb("stats", [P, BLOCK_TILES, 6])
        meanvar = sb("meanvar", [P, TILES, 2])
        rstd = sb("rstd", [P, TILES])
        minus_half = sb("minus_half", [P, TILES])
        attn_hi = sb("attn_hi", [P, GROUP, BLOCK], F32R)
        attn_lo = sb("attn_lo", [P, GROUP, BLOCK], F32R)
        pT_hi = sb("pT_hi", [P, 2, ROWS], F32R)
        pT_lo = sb("pT_lo", [P, 2, ROWS], F32R)

        ident = tab[:, T_IDENT:T_IDENT + P]

        bank_a = pb("bank_a", [P, 512])
        bank_b = pb("bank_b", [P, 512])
        s_ps = pb("s_ps", [P, 2, 512])
        t_ps = pb("t_ps", [P, 2, 512])
        pv_ps = pb("pv_ps", [P, 512])
        o_ps = pb("o_ps", [P, 512])

        landing = [raw[:, 0, :], raw[:, 1, :], v_T[:, :], probs[:, :, :].rearrange("p h k -> p (h k)")[:, 0:512]]

        first_banks = [t_ps[:, 0, :], t_ps[:, 1, :], pv_ps[:, :], o_ps[:, :]]

        tables_in = sem("tables_in")
        x_in = [sem(f"x_in{b}") for b in range(BLOCKS)]
        x0_in = [sem(f"x0_in{t}") for t in range(BLOCK_TILES)]
        ar_in = sem("ar_in")
        bT_in = sem("bT_in")
        stat_done = sem("stat_done")
        aggr_done = sem("aggr_done")
        vareps_done = sem("vareps_done")
        half_done = sem("half_done")
        rstd_done = sem("rstd_done")
        norm_done = sem("norm_done")
        xpose_done = sem("xpose_done")
        xhi_done = sem("xhi_done")
        xlo_done = sem("xlo_done")
        arhi_done = sem("arhi_done")
        ar_done = sem("ar_done")
        gate_step = sem("gate_step")
        gate_shift = sem("gate_shift")
        gate_exp = sem("gate_exp")
        gm_done = sem("gm_done")
        side_ps = sem("side_ps")
        side_out = sem("side_out")
        tanh_done = sem("tanh_done")
        gate_out = [sem(f"gate_out{i}") for i in range(2)]
        raw_in = [sem(f"raw_in{i}") for i in range(2)]
        whi_done = sem("whi_done")
        zero_done = sem("zero_done")
        w_ready = [sem(f"w_ready{c}") for c in range(CHUNKS)]
        proj_done = [sem(f"proj_done_{k}") for k in KINDS + ["v", "vt0", "vt1"]]
        rot_done = [sem(f"rot_done_{k}") for k in KINDS]
        sin_done = [sem(f"sin_done_{k}") for k in KINDS]
        cos_done = [sem(f"cos_done_{k}") for k in KINDS]
        sum_done = [sem(f"sum_done_{k}") for k in KINDS]
        qhi_done = [sem(f"qhi_done_{k}") for k in KINDS]
        q_ready = [sem(f"q_ready_{k}") for k in KINDS]
        khi1_done = sem("khi1_done")
        k1_ready = sem("k1_ready")
        vT_done = sem("vT_done")
        vhi_done = [sem(f"vhi_done{b}") for b in range(2)]
        v_ready = [sem(f"v_ready{b}") for b in range(2)]
        scores_done = sem("scores_done")
        hilo_done = sem("hilo_done")
        early_done = sem("early_done")
        ratio_done = sem("ratio_done")
        masked_done = sem("masked_done")
        exp_done = sem("exp_done")
        inv_done = sem("inv_done")
        probs_ready = sem("probs_ready")
        pT_ps = sem("pT_ps")
        pThi_done = sem("pThi_done")
        pT_ready = sem("pT_ready")
        pv_done = sem("pv_done")
        attnhi_done = sem("attnhi_done")
        attn_ready = sem("attn_ready")
        o_done = sem("o_done")
        y_added = sem("y_added")
        y_cleared = sem("y_cleared")
        xg_in = sem("xg_in")
        late_in = [sem(f"late_in{i}") for i in range(3)]
        y_gated = sem("y_gated")
        y_final = sem("y_final")
        out_done = sem("out_done")

        X_FIRST = 2 * BLOCK_TILES
        THROUGH = ("x", "ar", "mt", "gt", "d")
        steps = [("x", t) for t in range(X_FIRST, TILES)]
        for b in range(BLOCKS):
            steps += [("ar", b), ("mt", b)]
        steps += [("route", 0), ("exp", 0), ("route", 1)]
        for b in range(BLOCKS):
            steps += [("gt", b)] + [("d", BLOCK_TILES * b + t) for t in range(BLOCK_TILES)]
        places = [(0, 1, 3)] + [(0, j, p) for j in (2, 3) for p in (0, 1, 3)]
        places += [(1, j, p) for j in range(4) for p in ((0, 1, 3), (0, 3), (1, 3), (0, 1, 3))[j]]
        places += [(2, 0, 1), (2, 0, 2), (2, 0, 3), (2, 1, 0), (2, 1, 2), (2, 1, 3), (2, 2, 1), (2, 2, 3)]
        places += [(2, 3, p) for p in range(4)] + [(3, 0, p) for p in range(4)]
        places += [(3, 1, 0), (3, 1, 3), (3, 2, 1), (3, 2, 3), (3, 3, 0), (3, 3, 1)]
        side_plan, through_ps = {}, 0
        for place, (what, i) in zip(places, steps):
            side_plan[place] = (what, i, through_ps)
            through_ps += what in THROUGH
        assert len(places) >= len(steps)

        SIDE_X = TILES - X_FIRST

        def side_uses(u, j, p):
            return sum(1 for at, (what, _, _) in side_plan.items() if at < (u, j, p) and what in THROUGH)

        def wait_side(eng, uses):
            if uses > SIDE_X:
                eng.wait_ge(side_out, uses - SIDE_X)
            elif uses:
                eng.wait_ge(xlo_done, X_FIRST + uses)

        silu_at = {i: before + 1 - SIDE_X for what, i, before in side_plan.values() if what == "d"}

        def side_at(u, j, p):
            return side_plan.get((u, j, p)) if isinstance(u, int) else None

        late_xg = [(k_full[:, :], v_T[:, :])] + [(rot[:, i, :], cosx[:, i, :]) for i in range(2)]
        late_banks = [bank_a, bank_b, s_ps[:, 0, :]]

        block = ctx.enter_context(nc.Block())
        FINAL = UNITS - BLOCKS
        LAST = UNITS - 1

        def slots(eng, u):
            return {c: (4 * u + c if isinstance(u, int) else eng.snap(4 * u + c)) for c in range(-4, 6)}

        def units(eng, u):
            return [u + c if isinstance(u, int) or c == 0 else eng.snap(u + c) for c in range(3)]

        def is_unit(u, n):
            return isinstance(u, int) and u == n

        def value(eng, v):
            return v if isinstance(v, int) else eng.snap(v)

        @block.sync
        def _(sp):
            for t in range(BLOCK_TILES):
                sp.dma_start(x_sb[:, t, :], x_t[t, :, :]).then_inc(x0_in[t], 16)
            for c in range(len(landing)):
                sp.dma_start(landing[c], w_seq[c, :, :]).then_inc(raw_in[c % 2], 16)
            for b in range(1, BLOCKS):
                sp.dma_start(x_sb[:, BLOCK_TILES * b:BLOCK_TILES * (b + 1), :],
                             x_t[BLOCK_TILES * b:BLOCK_TILES * (b + 1), :, :].rearrange("t p d -> p t d"))\
                  .then_inc(x_in[b], 16)
            for c in range(len(landing), WO + 2):
                before = c - len(landing) if c < WO else c - 2
                sp.wait_ge(w_ready[before], 1)
                sp.dma_start(raw[:, c % 2, :], w_seq[c, :, :]).then_inc(raw_in[c % 2], 16)
            sp.wait_ge(xpose_done, -(-AR_END // DM))
            sp.dma_start(ar_raw[:, :, :], a_r).then_inc(ar_in, 16)

            def load_chunk(g, c):
                before = (c - 2) % CHUNKS
                sp.wait_ge(w_ready[before], value(sp, g + 1 if c >= 2 else g))
                sp.dma_start(raw[:, c % 2, :], w_seq[value(sp, g * CHUNKS + c), :, :]).then_inc(raw_in[c % 2], 16)

            with sp.Fori(0, KV_HEADS - 1) as g:
                for c in range(WO + 2, CHUNKS):
                    load_chunk(g, c)
                g_next = sp.snap(g + 1)
                for c in range(WO + 2):
                    load_chunk(g_next, c)
            for c in range(WO + 2, CHUNKS):
                load_chunk(KV_HEADS - 1, c)
            for r in range(2):
                sp.wait_ge(gate_out[r], 16 * TILES // 2)
            for c in range(CHUNKS - 2, CHUNKS):
                sp.wait_ge(w_ready[c], KV_HEADS)

            def load_xg(t):
                sp.dma_start(raw[:, 0, :], x_t[t, :, :]).then_inc(xg_in, 16)
                sp.dma_start(raw[:, 1, :], g_dram[t, :, :]).then_inc(xg_in, 16)

            def store_tile(t):
                sp.wait_ge(y_final, value(sp, t + 1))
                sp.dma_start(out_t[t, :, :], y_sum[:, t, :]).then_inc(out_done, 16)

            with sp.Fori(0, TILES - 4) as t:
                load_xg(t)
                store_tile(t)
            load_xg(TILES - 4)
            sp.wait_ge(q_ready[H3], UNITS)
            sp.wait_ge(proj_done[VT1], UNITS)
            for i in range(3):
                for dst, src in zip(late_xg[i], (x_t, g_dram)):
                    sp.dma_start(dst, src[TILES - 3 + i, :, :]).then_inc(late_in[i], 16)
            for t in range(TILES - 4, TILES):
                store_tile(t)
            sp.wait_ge(out_done, 16 * TILES)

        @block.gpsimd
        def _(pool):
            nc.gpsimd.memset(minus_half[:, :], -0.5).then_inc(half_done, 1)
            nc.gpsimd.memset(zero[:, :], 0.0).then_inc(zero_done, 1)
            pool.wait_ge(half_done, 1)
            pool.wait_ge(zero_done, 1)

            def inverse_std(b, t=None):
                s = slice(BLOCK_TILES * b, BLOCK_TILES * (b + 1)) if t is None else slice(t, t + 1)
                pool.wait_ge(vareps_done, BLOCK_TILES + b if t is None else t + 1)
                nc.gpsimd.tensor_tensor(rstd[:, s], meanvar[:, s, 1], minus_half[:, s], ALU.pow).then_inc(rstd_done, 1)

            def split(g, c):
                r = c % 2
                pool.wait_ge(raw_in[r], value(pool, 16 * (CHUNKS // 2 * g + c // 2 + 1)))
                nc.gpsimd.tensor_tensor(w_hi[:, c, :], raw[:, r, :], zero[:, 0:1].to_broadcast([P, 512]),
                                        ALU.add).then_inc(whi_done, 1)
                pool.wait_ge(whi_done, value(pool, CHUNKS * g + c + 1))
                nc.gpsimd.tensor_tensor(w_lo[:, c, :], raw[:, r, :], w_hi[:, c, :].bitcast(F32),
                                        ALU.subtract).then_inc(w_ready[c], 1)

            def sin_product(kind, count):
                s = T_SINK if kind == K else T_SINQ
                v = rot[:, BUF[kind], :].rearrange("p (b t) -> p b t", b=2)
                pool.wait_ge(rot_done[kind], count)
                nc.gpsimd.tensor_tensor(v, v, tab[:, s:s + SEQ].unsqueeze(1).to_broadcast([P, 2, SEQ]),
                                        ALU.mult).then_inc(sin_done[kind], 1)

            def first_low(c):
                src = landing[c] if c < len(landing) else raw[:, c % 2, :]
                pool.wait_ge(whi_done, c + 1)
                nc.gpsimd.tensor_tensor(w_lo[:, c, :], src, w_hi[:, c, :].bitcast(F32), ALU.subtract)\
                    .then_inc(w_ready[c], 1)

            for t in range(BLOCK_TILES):
                inverse_std(0, t)
            for c in range(WQ + 2):
                first_low(c)
            inverse_std(1)
            first_low(WQ + 2)
            pool.wait_ge(tables_in, 16)
            sin_product(K, 1)
            sin_product(H0, 1)
            first_low(WQ + 3)
            sin_product(H1, 1)
            first_low(WV)
            sin_product(H2, 1)

            def add_residual(t):
                y = y_sum[:, t, :]
                pool.wait_ge(y_gated, t + 1)
                nc.gpsimd.tensor_tensor(y, y, raw[:, 0, :], ALU.add).then_inc(y_final, 1)

            def group(g, g_next):
                u0 = value(pool, 4 * g)
                for i in range(BLOCKS):
                    last = g_next is None and i == BLOCKS - 1
                    own = value(pool, u0 + i + 1)
                    ahead = None if last else value(pool, u0 + i + 2)
                    for j in range(4):
                        if g_next is None and 4 * i + j > 3:
                            add_residual(4 * i + j - 4)
                        if j == 0:
                            sin_product(H3, own)
                        if i == 0 and j == 2:
                            pool.wait_ge(proj_done[VT1], own)
                            split(g, WO)
                            split(g, WO + 1)
                        if j > 0 and not last:
                            sin_product((K, H0)[j - 1] if j < 3 else H1, ahead)
                        if is_unit(g, 0) and i == 0 and j < 2:
                            inverse_std(2 + j)
                        if i == 0 and j == 2:
                            split(g, WO + 2)
                        if i == 0 and j == 3:
                            split(g, WO + 3)
                        if j == 3 and not last:
                            sin_product(H2, ahead)
                        if g_next is None:
                            continue
                        used = value(pool, 4 * g + 4) if (i, j) in ((2, 2), (2, 3), (3, 0), (3, 1), (3, 2)) else None
                        if (i, j) == (2, 2):
                            pool.wait_ge(proj_done[K], used)
                            split(g_next, WK)
                        elif (i, j) in ((2, 3), (3, 0), (3, 1)):
                            h = {(2, 3): 0, (3, 0): 1, (3, 1): 2}[i, j]
                            pool.wait_ge(proj_done[H0 + h], used)
                            split(g_next, WQ + h)
                        elif (i, j) == (3, 2):
                            pool.wait_ge(proj_done[H3], used)
                            split(g_next, WQ + 3)
                            pool.wait_ge(proj_done[V], used)
                            split(g_next, WV)

            group(0, 1)
            with pool.Fori(1, KV_HEADS - 1) as g:
                group(g, pool.snap(g + 1))
            group(KV_HEADS - 1, None)
            add_residual(TILES - 4)

        def three_pass(dst, w, x0):
            for c in range(DC):
                for n, (a, x) in enumerate(((0, xT_hi), (0, xT_lo), (1, xT_hi))):
                    mm = nc.tensor.matmul(dst, w(a, c), x[:, c, bass.ds(x0, BLOCK)], start=(c == 0 and n == 0),
                                          stop=(c == DC - 1 and n == 2))
            return mm

        def turn_x(t, bank):
            nc.tensor.wait_ge(norm_done, t + 1)
            for c in range(DC):
                mm = nc.tensor.transpose(bank[:, c * P:(c + 1) * P], x_sb[:, t, c * P:(c + 1) * P], ident)
            return mm.then_inc(xpose_done, 1)

        def pe_side(u, j, p):
            side = side_at(u, j, p)
            if side is None:
                return
            pe = nc.tensor
            what, i, before = side
            if what not in THROUGH:
                return
            tiles = max(0, 4 * u + j - 3 + (p > 1 or j == 2))
            if tiles:
                pe.wait_ge(y_added, tiles)
            wait_side(pe, before)
            t0 = BLOCK_TILES * i
            if what == "x":
                pe.wait_ge(norm_done, i + 1)
                for c in range(DC):
                    mm = nc.tensor.transpose(o_ps[:, c * P:(c + 1) * P], x_sb[:, i, c * P:(c + 1) * P], ident)
                mm.then_inc(xpose_done, 1)
            elif what == "ar":
                if i == 0:
                    pe.wait_ge(ar_done, 1)
                    pe.wait_ge(xlo_done, TILES)
                three_pass(o_ps[0:AR, :], lambda w, c: (ar_hi, ar_lo)[w][:, c, :], BLOCK * i).then_inc(side_ps, 1)
            elif what == "mt":
                for t in range(BLOCK_TILES):
                    mm = nc.tensor.transpose(o_ps[:, AR * t:AR * (t + 1)], mid_T[:, t * P:(t + 1) * P],
                                             ident[0:AR, 0:AR])
                mm.then_inc(side_ps, 1)
            elif what == "gt":
                if i == 0:
                    pe.wait_ge(gm_done, 1)
                    pe.wait_ge(bT_in, 16)
                for t in range(BLOCK_TILES):
                    mm = nc.tensor.transpose(o_ps[0:EXPERTS * RANK, t * P:(t + 1) * P],
                                             mid[:, t0 + t, 0:EXPERTS * RANK], ident)
                mm.then_inc(side_ps, 1)
            else:
                t = i % BLOCK_TILES
                nc.tensor.matmul(o_ps[:, :], gm_T[:, t * P:(t + 1) * P], bT[:, :], start=True, stop=True)\
                    .then_inc(side_ps, 1)

        def project(kind, bank, chunk, x0, weights):
            nc.tensor.wait_ge(w_ready[chunk], weights)
            three_pass(bank[:, :], lambda w, c: (w_hi, w_lo)[w][:, chunk, c * P:(c + 1) * P], x0)\
                .then_inc(proj_done[kind], 1)

        def scores(b, hp):
            k0, k1 = slice(SEQ * b, SEQ * b + P), slice(SEQ * b, SEQ * b + SEQ)
            for h in range(2):
                head = 2 * hp + h
                nc.tensor.matmul(s_ps[:, h, 0:2 * P].rearrange("p (s k) -> p s k", s=2), q_hi[:, head, k0],
                                 k_parts[:, :, k0], start=True, stop=False)
                nc.tensor.matmul(s_ps[:, h, 0:P], q_lo[:, head, k0], k_hi[:, k0], start=False, stop=True)
                late = slice(SEQ * b + P, SEQ * b + SEQ)
                for n, (a, k) in enumerate(((q_hi, k_hi), (q_hi, k_lo), (q_lo, k_hi))):
                    mm = nc.tensor.matmul(s_ps[:, h, 2 * P:], a[:, head, late], k[:, k1], start=(n == 0), stop=(n == 2))
            mm.then_inc(scores_done, 1)

        def prob_value(at, j, v_count, first_items=False):
            pe = nc.tensor
            b = ((j - 1) % 4) // 2
            pe.wait_ge(pT_ready, at(0))
            pe.wait_ge(v_ready[b], v_count)
            if not first_items:
                pe.wait_ge(attn_ready, at(-1))
            full = pv_ps[:, :].rearrange("p (h q) -> p h q", h=2)
            steps = [(full, v_hi, 0, pT_hi, 0), (full[:, :, P:], v_hi, 1, pT_hi, SEQ), (full[:, :, P:], v_hi, 1, pT_lo, SEQ),
                     (full[:, :, P:], v_lo, 1, pT_hi, SEQ), (full, v_hi, 0, pT_lo, 0), (full, v_lo, 0, pT_hi, 0)]
            for i, (dst, v, kb, p, c) in enumerate(steps):
                mm = nc.tensor.matmul(dst, v[:, 2 * b + kb, :], p[:, :, c:c + (P if kb else SEQ)], start=(i == 0), stop=(i == 5))
            mm.then_inc(pv_done, 1)

        def output_heads(b, t, bank, heads, weights=None):
            rows = slice(SEQ * b + P * t, SEQ * b + P * (t + 1))
            for h in heads:
                if weights is not None:
                    nc.tensor.wait_ge(w_ready[WO + h], weights)
                for i, (a, w) in enumerate(((attn_hi, w_hi), (attn_hi, w_lo), (attn_lo, w_hi))):
                    mm = nc.tensor.matmul(bank[:, :], a[:, h, rows], w[:, WO + h, :], start=(h == 0 and i == 0),
                                          stop=(h == GROUP - 1 and i == 2))
            return mm

        def output_tile(at, j, first_tile=False, bank=o_ps, weights=None):
            pe = nc.tensor
            b, t = ((j - 3) % 4) // 2, ((j - 3) % 4) % 2
            pe.wait_ge(attn_ready, at(-1 if t == 0 else -2))
            if not first_tile and bank is o_ps:
                pe.wait_ge(y_added, at(-3))
            output_heads(b, t, bank, range(GROUP), weights).then_inc(o_done, 1)

        def pe_unit(u):
            pe = nc.tensor
            first, last = is_unit(u, 0), is_unit(u, LAST)
            c0, c1, c2 = units(pe, u)
            n4 = slots(pe, u)
            x_own = value(pe, (u % BLOCKS) * BLOCK)
            x_next = value(pe, ((u + 1) % BLOCKS) * BLOCK)
            w_own = value(pe, u // BLOCKS + 1)
            w_next = value(pe, (u + 1) // BLOCKS + 1)
            for j in range(4):
                n = n4[j]

                def tile_out():
                    if first and j < 3:
                        return
                    if isinstance(u, int) and u < BLOCKS:
                        wait_side(pe, side_uses(u, j, 2 if j != 2 else 0))
                    output_tile(lambda c: n4[j + c], j, first_tile=first, weights=w_own if j == 3 else None)

                if j == 2:
                    tile_out()
                pe_side(u, j, 0)
                if j == 0:
                    pe.wait_ge(cos_done[H2], c1)
                    pe.wait_ge(cos_done[H1], c1)
                    project(H3, bank_a, WQ + 3, x_own, w_own)
                    pe_side(u, j, 1)
                    project(V, bank_b, WV, x_own, w_own)
                elif j in (1, 2):
                    pe.wait_ge(vT_done, c1)
                    if j == 1:
                        pe.wait_ge(cos_done[H3], c1)
                    else:
                        pe.wait_ge(v_ready[0], c1)
                    for kb in range(2):
                        t = 2 * (j - 1) + kb
                        mm = nc.tensor.transpose(bank_a[:, kb * P:(kb + 1) * P], v_T[:, t * P:(t + 1) * P], ident)
                    mm.then_inc(proj_done[VT0 if j == 1 else VT1], 1)
                    if not last:
                        if j == 1:
                            if isinstance(u, int) and u < BLOCKS - 1:
                                pe.wait_ge(xlo_done, BLOCK_TILES * (u + 2))
                            project(K, bank_b, WK, x_next, w_next)
                        else:
                            pe.wait_ge(cos_done[K], c2)
                            project(H0, bank_b, WQ, x_next, w_next)
                    pe_side(u, j, 1)
                elif not last:
                    pe.wait_ge(v_ready[1], c1)
                    project(H1, bank_a, WQ + 1, x_next, w_next)
                    pe_side(u, j, 1)
                    pe.wait_ge(cos_done[H0], c2)
                    project(H2, bank_b, WQ + 2, x_next, w_next)
                if j != 2:
                    tile_out()
                if not (first and j == 0):
                    prob_value(lambda c: n4[j + c], j, v_count=c1 if j > 0 else c0, first_items=first and j == 1)
                pe_side(u, j, 2)
                if last and j == 3:
                    pe.wait_ge(v_ready[1], c1)
                    output_tile(lambda c: n + 1 + c, 0, bank=bank_a)
                pe.wait_ge(probs_ready, n4[j + 1])
                if not (first and j == 0):
                    pe.wait_ge(pT_ready, n)
                for h in range(2):
                    for s in range(ROWS // P):
                        mm = nc.tensor.transpose(t_ps[:, h, s * P:(s + 1) * P], probs[:, h, s * P:(s + 1) * P], ident)
                mm.then_inc(pT_ps, 1)
                pe_side(u, j, 3)
                if not (last and j == 3):
                    pe.wait_ge(masked_done, n4[j + 1])
                    if j == 0:
                        pe.wait_ge(q_ready[H2], c1)
                        pe.wait_ge(q_ready[H3], c1)
                    elif j == 1:
                        pe.wait_ge(k1_ready, c1)
                    elif j == 3:
                        for kind in (K, H0, H1):
                            pe.wait_ge(q_ready[kind], c2)
                    scores(b=((j + 1) % 4) // 2, hp=(j + 1) % 2)

        @block.tensor
        def _(pe):
            pe.wait_ge(tables_in, 16)


            def keep_clock(columns, times):
                for _ in range(times):
                    nc.tensor.matmul(s_ps[:, 0, 0:columns], ident, tab[:, 0:columns], start=True, stop=True)

            keep_clock(512, 2)
            for t in range(BLOCK_TILES):
                turn_x(t, first_banks[t])
                keep_clock(P, 2)
            keep_clock(512, 1)
            pe.wait_ge(xlo_done, BLOCK_TILES)
            project(K, bank_b, WK, 0, 1)
            project(H0, bank_a, WQ, 0, 1)
            pe.wait_ge(cos_done[K], 1)
            project(H1, bank_b, WQ + 1, 0, 1)
            pe.wait_ge(cos_done[H0], 1)
            project(H2, bank_a, WQ + 2, 0, 1)
            for t in range(BLOCK_TILES, 2 * BLOCK_TILES):
                turn_x(t, first_banks[t % BLOCK_TILES])
            for kind in (K, H0, H1):
                pe.wait_ge(q_ready[kind], 1)
            scores(0, 0)
            for u in range(BLOCKS):
                pe_unit(u)
            with pe.Fori(BLOCKS, LAST) as u:
                pe_unit(u)
            pe_unit(LAST)
            n = 4 * UNITS
            pe.wait_ge(attn_ready, n - 1)
            output_heads(1, 0, late_banks[1], range(0, 2))
            prob_value(lambda c: n + c, 0, v_count=UNITS)
            output_heads(1, 1, late_banks[2], range(0, 2))
            pe.wait_ge(attn_ready, n)
            for t in range(2):
                output_heads(1, t, late_banks[1 + t], range(2, GROUP)).then_inc(o_done, 1)

        def x_high(t, bank):
            nc.scalar.wait_ge(xpose_done, t + 1)
            nc.scalar.activation(xT_hi[:, :, t * P:(t + 1) * P], bank.rearrange("p (c t) -> p c t", c=DC),
                                 ACT.Copy).then_inc(xhi_done, 1)

        def store_silu(t):
            nc.scalar.wait_ge(side_out, silu_at[t])
            nc.scalar.dma_start(g_dram[t, :, :], silu[:, t % 2, :]).then_inc(gate_out[t % 2], 16)

        def act_side(u, j, p):
            side = side_at(u, j, p)
            if side is None:
                return
            act = nc.scalar
            what, i, before = side
            if what == "x":
                x_high(i, o_ps[:, :])
                if i == TILES - 1:
                    nc.scalar.wait_ge(xpose_done, TILES)
                    nc.scalar.dma_start(bT[:, :], b_t).then_inc(bT_in, 16)
            elif what == "ar":
                act.wait_ge(side_ps, before + 1 - SIDE_X)
                nc.scalar.activation(mid_T[:, :], o_ps[0:AR, :], ACT.Copy).then_inc(side_out, 1)
            elif what == "exp":
                act.wait_ge(gate_shift, 1)
                nc.scalar.activation(gate[:, :, :], gate[:, :, :], ACT.Exp).then_inc(gate_exp, 1)
            elif what == "gt":
                act.wait_ge(side_ps, before + 1 - SIDE_X)
                nc.scalar.activation(gm_T[:, :], o_ps[0:EXPERTS * RANK, :], ACT.Copy).then_inc(side_out, 1)
            elif what == "d":
                if i >= 1:
                    store_silu(i - 1)
                act.wait_ge(side_ps, before + 1 - SIDE_X)
                if i >= 2:
                    act.wait_ge(gate_out[i % 2], 16 * (i // 2))
                nc.scalar.activation(silu[:, i % 2, :], o_ps[:, :], ACT.Tanh).then_inc(tanh_done, 1)

        def swap_halves(kind, bank, count, before, before_count):
            act = nc.scalar
            act.wait_ge(proj_done[kind], count)
            if before is not None:
                act.wait_ge(sum_done[before], before_count)
            r = rot[:, BUF[kind], :]
            half = HD // 2
            nc.scalar.activation(r[0:half, :], bank[half:HD, :], ACT.Copy)
            nc.scalar.activation(r[half:HD, :], bank[0:half, :], ACT.Copy).then_inc(rot_done[kind], 1)

        def q_high(kind, count, used):
            act = nc.scalar
            act.wait_ge(sum_done[kind], count)
            if used is not None:
                act.wait_ge(scores_done, used)
            nc.scalar.activation(q_hi[:, kind - H0, :], cosx[:, BUF[kind], :], ACT.Copy).then_inc(qhi_done[kind], 1)

        def k_high(b, count, used):
            act = nc.scalar
            act.wait_ge(sum_done[K], count)
            if used is not None:
                act.wait_ge(scores_done, used)
            s = slice(SEQ * b, SEQ * (b + 1))
            nc.scalar.activation(k_hi[:, s], k_full[:, s], ACT.Copy).then_inc((qhi_done[K], khi1_done)[b], 1)

        def v_high(b, count, used):
            act = nc.scalar
            act.wait_ge(proj_done[VT0 + b], count)
            if used is not None:
                act.wait_ge(pv_done, used)
            nc.scalar.activation(v_hi[:, 2 * b:2 * b + 2, :], bank_a[:, 0:SEQ].rearrange("p (k d) -> p k d", k=2),
                                 ACT.Copy).then_inc(vhi_done[b], 1)

        def attn_high(n, j, old=None):
            act = nc.scalar
            i = (j - 1) % 4
            act.wait_ge(pv_done, n)
            if old is not None:
                act.wait_ge(o_done, old)
            nc.scalar.activation(attn_hi[:, 2 * (i % 2):2 * (i % 2) + 2, SEQ * (i // 2):SEQ * (i // 2 + 1)],
                                 pv_ps[:, :].rearrange("p (h q) -> p h q", h=2), ACT.Copy).then_inc(attnhi_done, 1)

        def act_unit(u):
            act = nc.scalar
            first, last = is_unit(u, 0), is_unit(u, LAST)
            c0, c1, c2 = units(act, u)
            n4 = slots(act, u)
            for j in range(4):
                n = n4[j]
                act.wait_ge(scores_done, n4[j + 1])
                if first and j == 0:
                    act.wait_ge(w_ready[WQ + 2], 1)
                else:
                    act.wait_ge(pT_ps, n)
                nc.scalar.activation(probs[:, :, 0:P], s_ps[:, :, P:2 * P], ACT.Copy).then_inc(hilo_done, 1)
                act_side(u, j, 0)
                if j == 0:
                    q_high(H2, c1, None if first else n4[0])
                    swap_halves(H3, bank_a, c1, H2, c1)
                    act_side(u, j, 1)
                elif j == 1:
                    v_high(0, c1, None if first else n4[-2])
                elif j == 2 and not last:
                    k_high(0, c2, n4[2])
                elif j == 3 and not last:
                    q_high(H0, c2, n4[3])
                    k_high(1, c2, n4[4])
                    swap_halves(H1, bank_a, c2, K, c2)
                    act_side(u, j, 1)
                act.wait_ge(masked_done, n4[j + 1])
                for h in range(2):
                    for qt in range(2):
                        s = probs[:, h, P * qt:P * qt + P * (qt + 1)]
                        i = 2 * h + qt
                        a = nc.scalar.activation(s, s, ACT.Exp, bias=row_min[:, i:i + 1], scale=-1.0,
                                                 accum_out=row_sum[:, i:i + 1])
                a.then_inc(exp_done, 1)
                if j == 0:
                    act.wait_ge(proj_done[V], c1)
                    if not first:
                        act.wait_ge(proj_done[VT1], c0)
                    nc.scalar.activation(v_T[:, :], bank_b[:, :], ACT.Copy).then_inc(vT_done, 1)
                    q_high(H3, c1, None if first else n4[0])
                elif j == 1 and not last:
                    swap_halves(K, bank_b, c2, H1, c1)
                    act_side(u, j, 1)
                elif j == 2:
                    v_high(1, c1, None if first else n4[0])
                    if not last:
                        swap_halves(H0, bank_b, c2, H3, c1)
                        act_side(u, j, 1)
                elif j == 3 and not last:
                    swap_halves(H2, bank_b, c2, H0, c2)
                    q_high(H1, c2, n4[3])
                if is_unit(u, BLOCKS - 1) and j == 3:
                    store_silu(TILES - 1)
                if not (first and j == 0):
                    attn_high(n, j, None if first else n4[(-3, -2, -2, 0)[j]])
                act_side(u, j, 2)
                act.wait_ge(pT_ps, n4[j + 1])
                if not (first and j == 0):
                    act.wait_ge(pv_done, n)
                nc.scalar.activation(pT_hi[:, :, :], t_ps[:, :, 0:ROWS], ACT.Copy).then_inc(pThi_done, 1)
                act_side(u, j, 3)

        @block.scalar
        def _(act):
            nc.scalar.dma_start(tab[:, :], tables).then_inc(tables_in, 16)

            def first_high(c):
                src = landing[c] if c < len(landing) else raw[:, c % 2, :]
                nc.scalar.activation(w_hi[:, c, :], src, ACT.Copy).then_inc(whi_done, 1)

            for t in range(BLOCK_TILES - 1):
                x_high(t, first_banks[t])
            for i in range(2):
                act.wait_ge(raw_in[i], 32)
            first_high(WK)
            x_high(BLOCK_TILES - 1, first_banks[BLOCK_TILES - 1])
            for c in range(WQ, WQ + 3):
                first_high(c)
            swap_halves(K, bank_b, 1, None, None)
            act.wait_ge(raw_in[0], 48)
            first_high(WQ + 3)
            swap_halves(H0, bank_a, 1, None, None)
            k_high(0, 1, None)
            act.wait_ge(raw_in[1], 48)
            first_high(WV)
            q_high(H0, 1, None)
            swap_halves(H1, bank_b, 1, K, 1)
            q_high(H1, 1, None)
            swap_halves(H2, bank_a, 1, H0, 1)
            for t in range(BLOCK_TILES, 2 * BLOCK_TILES):
                x_high(t, first_banks[t % BLOCK_TILES])
            k_high(1, 1, None)
            for u in range(BLOCKS):
                act_unit(u)
            with act.Fori(BLOCKS, LAST) as u:
                act_unit(u)
            act_unit(LAST)
            attn_high(4 * UNITS, 0)

        def statistics(tiles, count):
            dve = nc.vector
            for t in tiles:
                ins = nc.vector.bn_stats(stats[:, t % BLOCK_TILES, :], x_sb[:, t, :])
            ins.then_inc(stat_done, 1)
            dve.wait_ge(stat_done, count)
            for t in tiles:
                ins = nc.vector.bn_aggr(meanvar[:, t, :], stats[:, t % BLOCK_TILES, :])
            ins.then_inc(aggr_done, 1)
            dve.wait_ge(aggr_done, count)
            s = slice(tiles[0], tiles[-1] + 1)
            nc.vector.tensor_scalar(meanvar[:, s, 1], meanvar[:, s, 1], EPS, None, ALU.add).then_inc(vareps_done, 1)

        def normalise(tiles, count):
            nc.vector.wait_ge(rstd_done, count)
            for t in tiles:
                nc.vector.tensor_scalar(x_sb[:, t, :], x_sb[:, t, :], meanvar[:, t, 0:1], rstd[:, t:t + 1],
                                        ALU.subtract, ALU.mult).then_inc(norm_done, 1)

        def block_statistics(b):
            nc.vector.wait_ge(x_in[b], 16)
            statistics(range(BLOCK_TILES * b, BLOCK_TILES * (b + 1)), BLOCK_TILES + b)

        def block_normalise(b):
            normalise(range(BLOCK_TILES * b, BLOCK_TILES * (b + 1)), BLOCK_TILES + b)

        def x_low(t, bank):
            s = slice(t * P, (t + 1) * P)
            nc.vector.wait_ge(xhi_done, t + 1)
            return nc.vector.tensor_tensor(xT_lo[:, :, s], bank.rearrange("p (c t) -> p c t", c=DC),
                                           xT_hi[:, :, s].bitcast(F32), ALU.subtract).then_inc(xlo_done, 1)

        def split_ar():
            dve = nc.vector
            dve.wait_ge(ar_in, 16)
            nc.vector.tensor_copy(ar_hi[:, :, :], ar_raw[:, :, :]).then_inc(arhi_done, 1)
            dve.wait_ge(arhi_done, 1)
            nc.vector.tensor_tensor(ar_lo[:, :, :], ar_raw[:, :, :], ar_hi[:, :, :].bitcast(F32), ALU.subtract)\
                .then_inc(ar_done, 1)

        def dve_side(u, j, p):
            side = side_at(u, j, p)
            if side is None:
                return
            dve = nc.vector
            what, i, before = side
            if what == "x":
                x_low(i, o_ps[:, :])
            elif what == "mt":
                dve.wait_ge(side_ps, before + 1 - SIDE_X)
                nc.vector.tensor_copy(mid[:, BLOCK_TILES * i:BLOCK_TILES * (i + 1), :],
                                      o_ps[:, 0:BLOCK_TILES * AR].rearrange("p (t r) -> p t r", r=AR))\
                    .then_inc(side_out, 1)
            elif what == "route":
                dve.wait_ge(side_out, before - SIDE_X)
                (route_choose, route_weigh)[i]()
            elif what == "d":
                dve.wait_ge(tanh_done, i + 1)
                nc.vector.scalar_tensor_tensor(out=silu[:, i % 2, :], in0=silu[:, i % 2, :], scalar=1.0,
                                               in1=o_ps[:, :], op0=ALU.add, op1=ALU.mult).then_inc(side_out, 1)

        wide = lambda v: v.unsqueeze(2).to_broadcast([P, TILES, EXPERTS])
        gate_steps = [0]

        def link(ins):
            gate_steps[0] += 1
            ins.then_inc(gate_step, 1)
            nc.vector.wait_ge(gate_step, gate_steps[0])

        def route_choose():
            logit = lambda e: mid[:, :, EXPERTS * RANK + e]
            pairs = [(0, 1), (0, 2), (0, 3), (1, 2), (1, 3), (2, 3)]
            c = {p: beats[:, i, :] for i, p in enumerate(pairs)}
            for a, b in pairs:
                ins = nc.vector.tensor_tensor(c[a, b], logit(a), logit(b), ALU.is_ge)
            link(ins)
            tt = nc.vector.tensor_tensor
            tt(keep[:, :, 0], c[0, 1], c[0, 2], ALU.add)
            tt(keep[:, :, 1], c[1, 2], c[1, 3], ALU.add)
            tt(keep[:, :, 2], c[2, 3], c[0, 2], ALU.subtract)
            link(tt(keep[:, :, 3], c[0, 3], c[1, 3], ALU.add))
            tt(keep[:, :, 0], keep[:, :, 0], c[0, 3], ALU.add)
            tt(keep[:, :, 1], keep[:, :, 1], c[0, 1], ALU.subtract)
            tt(keep[:, :, 2], keep[:, :, 2], c[1, 2], ALU.subtract)
            link(tt(keep[:, :, 3], keep[:, :, 3], c[2, 3], ALU.add))
            ts = nc.vector.tensor_scalar
            ts(keep[:, :, 0], keep[:, :, 0], 2.0, None, ALU.is_ge)
            ts(keep[:, :, 1], keep[:, :, 1], 0.5, None, ALU.is_ge)
            ts(keep[:, :, 2], keep[:, :, 2], -0.5, None, ALU.is_ge)
            ts(keep[:, :, 3], keep[:, :, 3], 1.5, None, ALU.is_lt)
            logits = mid[:, :, EXPERTS * RANK:AR]
            link(nc.vector.tensor_reduce(gmax[:, :], logits, AX.X, ALU.max))
            tt(gate[:, :, :], logits, wide(gmax[:, :]), ALU.subtract).then_inc(gate_shift, 1)

        def route_weigh():
            tt, ts = nc.vector.tensor_tensor, nc.vector.tensor_scalar
            nc.vector.wait_ge(gate_exp, 1)
            link(tt(gate[:, :, :], gate[:, :, :], keep[:, :, :], ALU.mult))
            link(nc.vector.tensor_reduce(gsum[:, :], gate[:, :, :], AX.X, ALU.add))
            link(nc.vector.reciprocal(gsum[:, :], gsum[:, :]))
            link(ts(gsum[:, :], gsum[:, :], LORA_SCALE / 2, None, ALU.mult))
            link(tt(gate[:, :, :], gate[:, :, :], wide(gsum[:, :]), ALU.mult))
            for e in range(EXPERTS):
                m = mid[:, :, RANK * e:RANK * (e + 1)]
                ins = tt(m, m, gate[:, :, e].unsqueeze(2).to_broadcast([P, TILES, RANK]), ALU.mult)
            ins.then_inc(gm_done, 1)

        def cos_product(kind, bank, count, old=None, old_count=None):
            s = T_COSK if kind == K else T_COSQ
            if old is not None:
                nc.vector.wait_ge(q_ready[old], old_count)
            nc.vector.wait_ge(rot_done[kind], count)
            nc.vector.tensor_tensor(cosx[:, BUF[kind], :].rearrange("p (b t) -> p b t", b=2),
                                    bank[:, :].rearrange("p (b t) -> p b t", b=2),
                                    tab[:, s:s + SEQ].unsqueeze(1).to_broadcast([P, 2, SEQ]),
                                    ALU.mult).then_inc(cos_done[kind], 1)

        def rotate(kind, count):
            nc.vector.wait_ge(sin_done[kind], count)
            nc.vector.wait_ge(cos_done[kind], count)
            dst = k_full[:, :] if kind == K else cosx[:, BUF[kind], :]
            nc.vector.tensor_tensor(dst, cosx[:, BUF[kind], :], rot[:, BUF[kind], :], ALU.add)\
                .then_inc(sum_done[kind], 1)

        def q_low(kind, count):
            nc.vector.wait_ge(qhi_done[kind], count)
            h = kind - H0
            nc.vector.tensor_tensor(q_lo[:, h, :], cosx[:, BUF[kind], :], q_hi[:, h, :].bitcast(F32), ALU.subtract)\
                .then_inc(q_ready[kind], 1)

        def k_low(b, count):
            nc.vector.wait_ge((qhi_done[K], khi1_done)[b], count)
            s = slice(SEQ * b, SEQ * (b + 1))
            nc.vector.tensor_tensor(k_lo[:, s], k_full[:, s], k_hi[:, s].bitcast(F32), ALU.subtract)\
                .then_inc((q_ready[K], k1_ready)[b], 1)

        def v_low(b, count):
            nc.vector.wait_ge(vhi_done[b], count)
            nc.vector.tensor_tensor(v_lo[:, 2 * b:2 * b + 2, :], bank_a[:, 0:SEQ].rearrange("p (k d) -> p k d", k=2),
                                    v_hi[:, 2 * b:2 * b + 2, :].bitcast(F32), ALU.subtract).then_inc(v_ready[b], 1)

        def attn_low(n, j):
            i = (j - 1) % 4
            nc.vector.wait_ge(attnhi_done, n)
            s = (slice(None), slice(2 * (i % 2), 2 * (i % 2) + 2), slice(SEQ * (i // 2), SEQ * (i // 2 + 1)))
            nc.vector.tensor_tensor(attn_lo[s], pv_ps[:, :].rearrange("p (h q) -> p h q", h=2),
                                    attn_hi[s].bitcast(F32), ALU.subtract).then_inc(attn_ready, 1)

        def turned_low(n):
            nc.vector.wait_ge(pThi_done, n)
            nc.vector.tensor_tensor(pT_lo[:, :, :], t_ps[:, :, 0:ROWS], pT_hi[:, :, :].bitcast(F32),
                                    ALU.subtract).then_inc(pT_ready, 1)

        def add_tile(at, tile, final=None, start=False, bank=o_ps, source=None):
            dve = nc.vector
            y = y_sum[:, tile, :]
            gate, residual, arrived, count = source or (raw[:, 1, :], raw[:, 0, :], xg_in,
                                                        None if final is None else value(dve, 32 * (final + 1)))
            dve.wait_ge(o_done, at(-2))
            if start:
                nc.vector.tensor_copy(y, o_ps[:, :]).then_inc(y_added, 1)
                return
            nc.vector.tensor_tensor(y, bank[:, :], y, ALU.add).then_inc(y_added, 1)
            if final is None:
                return
            dve.wait_ge(y_added, at(-2))
            dve.wait_ge(arrived, count)
            nc.vector.tensor_tensor(y, y, gate, ALU.mult).then_inc(y_gated, 1)
            if source is None:
                return
            dve.wait_ge(y_gated, value(dve, final + 1))
            dve.wait_ge(y_final, value(dve, final))
            nc.vector.tensor_tensor(y, y, residual, ALU.add).then_inc(y_final, 1)

        def dve_unit(u, final_from=4):
            dve = nc.vector
            first, last = is_unit(u, 0), is_unit(u, LAST)
            c0, c1, c2 = units(dve, u)
            n4 = slots(dve, u)
            tiles = [value(dve, (4 * u + (j + TILES - 3)) % TILES) for j in range(4)]
            for j in range(4):
                n = n4[j]

                def tile_in():
                    if not (first and j < 3):
                        add_tile(lambda c: n4[j + c], tiles[j], n4[j] - 3 - 4 * FINAL if j >= final_from else None,
                                 start=isinstance(u, int) and u < BLOCKS)

                if not (first and j <= 1):
                    attn_low(n4[j - 1], j - 1)
                dve.wait_ge(hilo_done, n4[j + 1])
                early = probs[:, :, 0:P]
                nc.vector.tensor_tensor(early, s_ps[:, :, 0:P], early, ALU.add).then_inc(early_done, 1)

                def masked(h, qt):
                    s = slice(P * qt, P * qt + P * (qt + 1))
                    i = 2 * h + qt
                    return nc.vector.tensor_tensor_reduce(
                        out=probs[:, h, s], in0=(probs[:, h, 0:P], s_ps[:, h, 2 * P:])[qt],
                        in1=tab[:, T_MASK + P * (1 - qt):T_MASK + SEQ], scale=1.0, scalar=MASKED,
                        op0=ALU.add, op1=ALU.min, accum_out=row_min[:, i:i + 1])

                masked(0, 1)
                dve.wait_ge(early_done, n4[j + 1])
                nc.vector.tensor_tensor(early, early, tab[:, T_RATIO:T_RATIO + P].unsqueeze(1).to_broadcast([P, 2, P]),
                                        ALU.mult).then_inc(ratio_done, 1)
                masked(1, 1)
                dve.wait_ge(tables_in, 16)
                dve.wait_ge(ratio_done, n4[j + 1])
                masked(0, 0)
                ins = masked(1, 0)
                ins.then_inc(masked_done, 1)
                dve_side(u, j, 0)
                if j == 0:
                    q_low(H2, c1)
                    if first:
                        for t in range(BLOCK_TILES, 2 * BLOCK_TILES):
                            x_low(t, first_banks[t % BLOCK_TILES])
                elif j == 2 and not last:
                    k_low(0, c2)
                elif j == 3 and not last:
                    q_low(H0, c2)
                if not (first and j == 0):
                    turned_low(n)
                if j == 1:
                    v_low(0, c1)
                elif j == 0:
                    cos_product(H3, bank_a, c1, H2, c1)
                    dve_side(u, j, 1)
                    rotate(H3, c1)
                elif j == 3 and not last:
                    k_low(1, c2)
                    cos_product(H1, bank_a, c2)
                    dve_side(u, j, 1)
                    rotate(H1, c2)
                dve.wait_ge(exp_done, n4[j + 1])
                nc.vector.reciprocal(row_inv[:, :], row_sum[:, :]).then_inc(inv_done, 1)
                dve.wait_ge(inv_done, n4[j + 1])
                for h in range(2):
                    for qt in range(2):
                        s = probs[:, h, P * qt:P * qt + P * (qt + 1)]
                        i = 2 * h + qt
                        ins = nc.vector.tensor_scalar(s, s, row_inv[:, i:i + 1], None, ALU.mult)
                ins.then_inc(probs_ready, 1)
                if j == 0:
                    q_low(H3, c1)
                    if first:
                        k_low(1, 1)
                        block_statistics(2)
                elif j == 1:
                    if not last:
                        cos_product(K, bank_b, c2, H1, c1)
                        dve_side(u, j, 1)
                        rotate(K, c2)
                    if first:
                        block_normalise(2)
                        block_statistics(3)
                elif j == 2:
                    tile_in()
                    if first:
                        block_normalise(3)
                    v_low(1, c1)
                    if not last:
                        cos_product(H0, bank_b, c2, H3, c1)
                        dve_side(u, j, 1)
                        rotate(H0, c2)
                elif not last:
                    cos_product(H2, bank_b, c2, H0, c2)
                    q_low(H1, c2)
                    rotate(H2, c2)
                if j != 2:
                    tile_in()
                dve_side(u, j, 2)
                dve_side(u, j, 3)
                if first and j == 3:
                    split_ar()

        @block.vector
        def _(dve):
            for t in range(BLOCK_TILES):
                dve.wait_ge(x0_in[t], 16)
                statistics([t], t + 1)
                if t > 0:
                    normalise([t - 1], t)
            normalise([BLOCK_TILES - 1], BLOCK_TILES)
            for t in range(BLOCK_TILES):
                x_low(t, first_banks[t])
            block_statistics(1)
            cos_product(K, bank_b, 1)
            block_normalise(1)
            cos_product(H0, bank_a, 1)
            rotate(K, 1)
            rotate(H0, 1)
            k_low(0, 1)
            q_low(H0, 1)
            cos_product(H1, bank_b, 1)
            rotate(H1, 1)
            q_low(H1, 1)
            cos_product(H2, bank_a, 1)
            rotate(H2, 1)
            for u in range(BLOCKS):
                dve_unit(u)
            for i in range(2):
                dve.wait_ge(gate_out[i], 16 * TILES // 2)
            nc.vector.memset(y_sum[:, TILES - 3:TILES, :], 0.0).then_inc(y_cleared, 1)
            dve.wait_ge(y_cleared, 1)
            with dve.Fori(BLOCKS, FINAL) as u:
                dve_unit(u)
            dve_unit(FINAL, final_from=3)
            with dve.Fori(FINAL + 1, LAST) as u:
                dve_unit(u, final_from=0)
            dve_unit(LAST, final_from=0)
            n = 4 * UNITS
            attn_low(n - 1, 3)
            turned_low(n)
            for i in range(3):
                if i == 1:
                    attn_low(n, 0)
                add_tile(lambda c: n + i + c, TILES - 3 + i, n + i - 3 - 4 * FINAL, bank=late_banks[i],
                         source=(late_xg[i][1], late_xg[i][0], late_in[i], 32))


def kernel(**inputs):
    import concourse.bacc as bacc
    from concourse.bass_utils import run_bass_kernel_spmd

    f32 = np.float32
    x = np.ascontiguousarray(inputs["L0_attn_hidden_states"]).reshape(TOKENS, DM)
    turn = lambda w: np.asarray(w).reshape(KV_HEADS, -1, HD, DC, P).transpose(0, 1, 4, 3, 2).reshape(KV_HEADS, -1, P, 512)
    wo = np.asarray(inputs["L0_attn_wo"]).T.reshape(KV_HEADS, GROUP, HD, DM)
    w_seq = np.ascontiguousarray(np.concatenate(
        [turn(inputs["L0_attn_wk"]), turn(inputs["L0_attn_wq"]), turn(inputs["L0_attn_wv"]), wo], axis=1)
        .reshape(KV_HEADS * CHUNKS, P, 512))
    ar = np.concatenate([np.asarray(inputs["L0_ffn_A"]).reshape(EXPERTS * RANK, DM),
                         np.asarray(inputs["L0_ffn_router_w"])], axis=0)
    a_r = np.ascontiguousarray(ar.reshape(AR, DC, P).transpose(2, 1, 0))
    b_t = np.ascontiguousarray(np.asarray(inputs["L0_ffn_B"]).transpose(0, 2, 1).reshape(EXPERTS * RANK, DM))

    inv_freq = (f32(1.0) / f32(ROPE_BASE) ** (np.arange(0, HD, 2, dtype=f32) / f32(HD))).astype(f32)
    pos = np.arange(SEQ)
    angle = np.concatenate([inv_freq, inv_freq])[:, None] * pos.astype(f32)[None, :]
    cos, sin = np.cos(angle).astype(f32), np.sin(angle).astype(f32)
    sin[:HD // 2] *= -1
    key_scale = np.where(pos < SYS_LEN, SUPPRESS, np.where(pos < SYS_LEN + IMG_LEN, ENHANCE, 1.0))
    fold = -key_scale / np.sqrt(HD)
    row, col = np.arange(P)[:, None], np.arange(P)[None, :]
    mask = np.concatenate([np.zeros((P, P)), np.where(col > row, MASKED, 0.0)], axis=1)
    ratio = np.where(row >= SYS_LEN + IMG_LEN, 1.0, 1.0 / key_scale[:P][None, :])
    tables = np.concatenate([cos, sin, cos * fold, sin * fold, mask, ratio, np.eye(P)], axis=1).astype(f32)

    arrays = {"x": x, "w_seq": w_seq, "a_r": a_r, "b_t": b_t, "tables": np.ascontiguousarray(tables)}
    nc = bacc.Bacc("TRN2", target_bir_lowering=False, num_devices=1)
    args = [nc.dram_tensor(name, a.shape, mybir.dt.from_np(a.dtype), kind="ExternalInput").ap()
            for name, a in arrays.items()]
    out = nc.dram_tensor("out", (TOKENS, DM), F32, kind="ExternalOutput").ap()
    build(nc, *args, out)
    r = run_bass_kernel_spmd(nc, [arrays], core_ids=[0])
    return r.results[0]["out"].reshape(BATCHES, SEQ, DM)
```
